# Optimizing a Trainium2 kernel written in Bass

```python
import numpy as np
import jax
import jax.numpy as jnp

def _softmax(x, axis=-1):
    return jax.nn.softmax(x, axis=axis)

def _gelu(x):
    return jax.nn.gelu(x, approximate=True)

def _silu(x):
    return jax.nn.silu(x)

def _sigmoid(x):
    return jax.nn.sigmoid(x)

def _layernorm(x, axis=-1, eps=1e-05):
    m = jnp.mean(x, axis=axis, keepdims=True)
    v = jnp.var(x, axis=axis, keepdims=True)
    return (x - m) / jnp.sqrt(v + eps)

def _scatter_add(tgt, idx, src, axis=0):
    return tgt.at[idx].add(src)

def _segment_sum(src, seg, n):
    return jax.ops.segment_sum(src, seg, n)
kernel_name = 'mk_adaln_d1_jaxref_r8_c25e7c'

def setup_inputs(seed: int=0):
    np.random.seed(seed)
    _w = jnp.asarray

    def _L0_attn_setup():
        import jax, jax.numpy as jnp
        import numpy as np
        import math
        N, S, E, H = (4, 512, 128, 16)
        D = E // H
        key = jax.random.key(seed)
        ks = jax.random.split(key, 9)
        w = 1.0 / math.sqrt(E)
        mk = lambda k, shape: jax.random.normal(k, shape, jnp.float32) * w
        return {'x': jax.random.normal(ks[0], (N, S, E), jnp.float32), 'Wq': mk(ks[1], (E, E)), 'bq': mk(ks[2], (E,)), 'Wk': mk(ks[3], (E, E)), 'bk': mk(ks[4], (E,)), 'Wv': mk(ks[5], (E, E)), 'bv': mk(ks[6], (E,)), 'Wo': mk(ks[7], (E, E)), 'bo': mk(ks[8], (E,))}
    _L0_attn_in = _L0_attn_setup()

    def _L0_ffn_setup():
        import jax, jax.numpy as jnp
        import numpy as np
        B, S, DIM = (4, 256, 128)
        E, K, HID = (8, 2, 512)
        key = jax.random.key(seed)
        ks = jax.random.split(key, 8)
        init = lambda k, sh: jax.random.normal(k, sh, jnp.float32) * 0.02
        return {'x': jax.random.normal(ks[0], (B, S, DIM), jnp.float32), 'gate_w': init(ks[1], (DIM, E)), 'gate_b': jnp.zeros((E,), jnp.float32), 'w1': init(ks[2], (E, DIM, HID)), 'b1': jnp.zeros((E, HID), jnp.float32), 'w2': init(ks[3], (E, HID, DIM)), 'b2': jnp.zeros((E, DIM), jnp.float32), 'ws1': init(ks[4], (DIM, HID)), 'bs1': jnp.zeros((HID,), jnp.float32), 'ws2': init(ks[5], (HID, DIM)), 'bs2': jnp.zeros((DIM,), jnp.float32)}
    _L0_ffn_in = _L0_ffn_setup()
    _L0_c = _w((lambda *s: np.random.randn(*s).astype(np.float32) * 0.05)(8, 128))
    _L0_wmod = _w((lambda *s: np.random.randn(*s).astype(np.float32) * 0.05)(128, 6 * 128) * 128 ** (-0.5))
    _d = {'L0_attn_x': _L0_attn_in['x'], 'L0_attn_Wq': _L0_attn_in['Wq'], 'L0_attn_bq': _L0_attn_in['bq'], 'L0_attn_Wk': _L0_attn_in['Wk'], 'L0_attn_bk': _L0_attn_in['bk'], 'L0_attn_Wv': _L0_attn_in['Wv'], 'L0_attn_bv': _L0_attn_in['bv'], 'L0_attn_Wo': _L0_attn_in['Wo'], 'L0_attn_bo': _L0_attn_in['bo'], 'L0_ffn_gate_w': _L0_ffn_in['gate_w'], 'L0_ffn_gate_b': _L0_ffn_in['gate_b'], 'L0_ffn_w1': _L0_ffn_in['w1'], 'L0_ffn_b1': _L0_ffn_in['b1'], 'L0_ffn_w2': _L0_ffn_in['w2'], 'L0_ffn_b2': _L0_ffn_in['b2'], 'L0_ffn_ws1': _L0_ffn_in['ws1'], 'L0_ffn_bs1': _L0_ffn_in['bs1'], 'L0_ffn_ws2': _L0_ffn_in['ws2'], 'L0_ffn_bs2': _L0_ffn_in['bs2'], 'L0_c': _L0_c, 'L0_wmod': _L0_wmod}
    _x0 = _d['L0_attn_x']
    _d['L0_attn_x'] = jax.random.normal(jax.random.fold_in(jax.random.key(seed), 1), (8, 1024, 128), dtype=_x0.dtype)
    del _x0
    return _d

def reference(L0_attn_x, L0_attn_Wq, L0_attn_bq, L0_attn_Wk, L0_attn_bk, L0_attn_Wv, L0_attn_bv, L0_attn_Wo, L0_attn_bo, L0_ffn_gate_w, L0_ffn_gate_b, L0_ffn_w1, L0_ffn_b1, L0_ffn_w2, L0_ffn_b2, L0_ffn_ws1, L0_ffn_bs1, L0_ffn_ws2, L0_ffn_bs2, L0_c, L0_wmod):

    def _L0_attn_ref(x, Wq, bq, Wk, bk, Wv, bv, Wo, bo):
        import jax, jax.numpy as jnp
        import numpy as np
        import math
        N, S, E, H = (4, 512, 128, 16)
        D = E // H
        n, s, e = x.shape
        h, d = (H, D)
        scale = 1.0 / math.sqrt(d)

        def proj(W, b):
            y = jnp.einsum('nse,fe->nsf', x, W) + b
            return y.reshape(n, s, h, d).transpose(0, 2, 1, 3)
        Q = proj(Wq, bq)
        K = proj(Wk, bk)
        V = proj(Wv, bv)
        scores = jnp.einsum('nqhd,nkhd->nhqk', Q, K) * scale
        attn = jax.nn.softmax(scores, axis=-1)
        out = jnp.einsum('nhql,nlhd->nqhd', attn, V)
        out = out.reshape(n, s, e)
        return jnp.einsum('nse,fe->nsf', out, Wo) + bo

    def _L0_ffn_ref(x, gate_w, gate_b, w1, b1, w2, b2, ws1, bs1, ws2, bs2):
        import jax, jax.numpy as jnp
        import numpy as np
        B, S, DIM = (4, 256, 128)
        E, K, HID = (8, 2, 512)
        orig_shape = x.shape
        xf = x.reshape(-1, DIM)
        logits = xf @ gate_w + gate_b
        top_w, top_i = jax.lax.top_k(logits, K)
        gw = jax.nn.softmax(top_w, axis=-1).astype(xf.dtype)
        combine = (gw[:, :, None] * jax.nn.one_hot(top_i, E, dtype=xf.dtype)).sum(axis=1)
        out = jnp.zeros_like(xf)
        for e in range(E):
            h = jax.nn.gelu(xf @ w1[e] + b1[e], approximate=False)
            out = out + combine[:, e:e + 1] * (h @ w2[e] + b2[e])
        shared = jax.nn.gelu(xf @ ws1 + bs1, approximate=False) @ ws2 + bs2
        return (out + shared).reshape(orig_shape)
    x = L0_attn_x
    mod = (_silu(L0_c) @ L0_wmod).reshape(L0_c.shape[0], 6, 1, -1)
    sa, ca, ga, sb, cb, gb = (mod[:, 0], mod[:, 1], mod[:, 2], mod[:, 3], mod[:, 4], mod[:, 5])
    ga = (2 * (ga >= 0) - 1) * jnp.maximum(jnp.abs(ga), 0.25)
    gb = (2 * (gb >= 0) - 1) * jnp.maximum(jnp.abs(gb), 0.25)
    h = _layernorm(x, axis=-1) * (1 + ca) + sa
    x = x + ga * _L0_attn_ref(h, L0_attn_Wq, L0_attn_bq, L0_attn_Wk, L0_attn_bk, L0_attn_Wv, L0_attn_bv, L0_attn_Wo, L0_attn_bo)
    h = _layernorm(x, axis=-1) * (1 + cb) + sb
    x = x + gb * _L0_ffn_ref(h, L0_ffn_gate_w, L0_ffn_gate_b, L0_ffn_w1, L0_ffn_b1, L0_ffn_w2, L0_ffn_b2, L0_ffn_ws1, L0_ffn_bs1, L0_ffn_ws2, L0_ffn_bs2)
    return x

_drawn_inputs = setup_inputs


def setup_inputs(seed=0):
    import zlib

    import numpy as np

    out = dict(_drawn_inputs(seed))
    spreads = {'L0_ffn_gate_b': (0.0, 0.568),
     'L0_ffn_b1': (0.0, 0.8),
     'L0_ffn_b2': (0.0, 0.475),
     'L0_ffn_bs1': (0.0, 0.8),
     'L0_ffn_bs2': (0.0, 0.337)}
    factors = {'L0_attn_bq': 8.0,
     'L0_attn_bk': 7.775,
     'L0_attn_bv': 7.572,
     'L0_ffn_gate_w': 3.375,
     'L0_ffn_w1': 5.98,
     'L0_ffn_w2': 5.471,
     'L0_ffn_ws1': 4.24,
     'L0_ffn_ws2': 3.907}
    for name, (base, spread) in spreads.items():
        noise = np.random.default_rng([zlib.crc32(name.encode()), seed]).standard_normal(out[name].shape)
        drawn = base * np.exp(spread * noise) if base else spread * noise
        out[name] = jnp.asarray(drawn.astype(out[name].dtype))
    for name, factor in factors.items():
        out[name] = (out[name] * factor).astype(out[name].dtype)
    return out
```

```python
from contextlib import ExitStack

import concourse.bass as bass
from concourse import mybir

F32 = mybir.dt.float32
ALU = mybir.AluOpType
ACT = mybir.ActivationFunctionType
AX = mybir.AxisListType

NB, S, E = 8, 1024, 128
P = 128
H, D = 16, 8
HH = H * H
C = S // P
CU = C // 2
SCALE = 1.0 / D ** 0.5
EPS = 1e-5
NX, HID = 8, 512
HC = HID // P
BT = 512


def flat(ap):
    return ap.rearrange("p a b -> p (a b)")


def need(engine, semaphore, count):
    if not isinstance(count, int) or count > 0:
        engine.wait_ge(semaphore, count)


def moments(nc, dve, stats, mean, tmp, var, ln_v, base, ready):
    total, gap, squares = tmp
    dve.wait_ge(ln_v, base)
    nc.vector.tensor_tensor(total, stats[:, :, 1], stats[:, :, 4], ALU.add)
    nc.vector.tensor_tensor(gap, stats[:, :, 1], stats[:, :, 4], ALU.subtract)
    nc.vector.tensor_tensor(squares, stats[:, :, 2], stats[:, :, 5], ALU.add).then_inc(ln_v, 1)
    dve.wait_ge(ln_v, base + 1)
    nc.vector.tensor_scalar(mean, total, 0.5, None, ALU.mult)
    nc.vector.scalar_tensor_tensor(gap, gap, 0.25, gap, ALU.mult, ALU.mult)
    nc.vector.tensor_scalar(squares, squares, 1.0 / E, EPS, ALU.mult, ALU.add).then_inc(ln_v, 1)
    dve.wait_ge(ln_v, base + 2)
    nc.vector.tensor_tensor(var, gap, squares, ALU.add).then_inc(ready, 1)


def attend(nc, io, scr, mod, ident, ps):
    with ExitStack() as ctx:
        sb = lambda n, s, d=F32: ctx.enter_context(nc.sbuf_tensor("attend_" + n, s, d))
        sem = lambda n: ctx.enter_context(nc.semaphore("attend_" + n))
        cT, sig, silu = sb("cT", [P, NB]), sb("sig", [P, NB]), sb("silu", [P, NB])
        wmod, raw = sb("wmod", [P, 6, E]), sb("raw_mod", [P, 6, NB])
        sgn, mag = sb("sgn", [P, 2, NB]), sb("mag", [P, 2, NB])
        wqkv, bqkv = sb("w_qkv", [P, 3 * E]), sb("b_qkv", [P, 3 * E])
        x = [sb(f"x{b}", [P, C, E]) for b in range(2)]
        stats, mean = sb("stats", [P, C, 6]), sb("mean", [P, C])
        tmp = [sb(f"moment_tmp{k}", [P, C])[:, :] for k in range(3)]
        var, std, rstd = sb("var", [P, C]), sb("std", [P, C]), sb("rstd", [P, C])
        shift = [sb(f"shift{b}", [P, 2, 1]) for b in range(2)]
        hT = sb("hT", [P, S])
        qkv = [sb(f"qkv{b}", [P, C, 3 * E]) for b in range(2)]
        QK_RING = CU
        qk_prod = [sb(f"qk_prod{r}", [P, D, H, H]) for r in range(QK_RING)]
        pv_pool = sb("pv_prod_pool", [P, H, H, D])
        DVE_PV = CU - 1
        pv_dve = [sb(f"pv_prod_dve{r}", [P, H, D, H]) for r in range(DVE_PV)]
        top, less = sb("row_max", [P, CU * H]), sb("less_max", [P, CU, HH])
        prob_sb = [sb(f"prob_last{g}", [P, HH]) for g in range(2)]
        total, recip = sb("row_sum", [P, CU * H]), sb("row_recip", [P, CU * H])
        sums = sb("sums", [P, DVE_PV, E])
        out = [sb(f"out{b}", [P, H, C, D]) for b in range(2)]

        small_in, wmod_in, exp_c, silu_v = sem("small_in"), sem("wmod_in"), sem("exp_neg_c"), sem("silu_v")
        mod_mm, mod_v = sem("mod_mm"), sem("mod_v")
        x_in = [sem(f"x_in{b}") for b in range(2)]
        ln_v, var_ready, std_ready = sem("ln_v"), sem("var_ready"), sem("std_ready")
        xn_ready, xt_mm, hT_done = sem("xn_ready"), sem("xt_mm"), sem("hT_done")
        qkv_mm, qkv_ready = sem("qkv_mm"), sem("qkv_ready")
        qk_prod_ready, qk_summed = sem("qk_prod_ready"), sem("qk_summed")
        top_v, less_v, prob_a, total_v, recip_v = (
            sem("row_max_v"), sem("less_max_v"), sem("prob_a"), sem("row_sum_v"), sem("row_recip_v"))
        pv_prod_ready, pv_summed = sem("pv_prod_ready"), sem("pv_summed")
        pv_mult_v, pv_sum_v, norm_v = sem("pv_mult_v"), sem("pv_sum_v"), sem("norm_v")
        stored = [sem(f"out_stored{b}") for b in range(2)]

        score = [ps[:, 2 * g:2 * g + 2, :].rearrange("p a (b s) -> p (a b) s", b=2) for g in range(2)]
        q_acc = [ps[:, 4 + j, 0:3 * E] for j in range(2)]
        t_acc, o_acc = ps[:, 6, :], ps[:, 7, 0:E]
        x_dram = io["x"].rearrange("n (p c) e -> n p c e", c=C)
        o_dram = scr["o"].rearrange("n h (p x) -> n p h x", p=P)
        block = ctx.enter_context(nc.Block())

        def steps(engine, batch):
            for b in range(2):
                batch(b, b)
            with engine.Fori(1, NB // 2 - 1) as i:
                for b in range(2):
                    batch(2 * i + b, b)
            for b in range(2):
                batch(NB - 2 + b, b, more=b == 0)

        @block.sync
        def _(sp):
            for dst, name in ((cT, "cT"), (wqkv, "w_qkv")):
                sp.dma_start(dst[:, :], io[name]).then_inc(small_in, 16)
            sp.dma_start(x[0][:, :, :], x_dram[0]).then_inc(x_in[0], 16)
            sp.dma_start(flat(wmod[:, :, :]), io["wmod"]).then_inc(wmod_in, 16)
            sp.dma_start(bqkv[:, :], io["b_qkv"].partition_broadcast(P)).then_inc(small_in, 16)
            sp.dma_start(x[1][:, :, :], x_dram[1]).then_inc(x_in[1], 16)

            def batch(t, b, more=True):
                if more:
                    sp.wait_ge(xt_mm, 2 * t + 2)
                    sp.dma_start(x[b][:, :, :], x_dram[t + 2]).then_inc(x_in[b], 16)
                sp.wait_ge(norm_v, 2 * t + 2)
                sp.dma_start(o_dram[t], out[b][:, :, :, :].rearrange("p h c d -> p h (c d)")).then_inc(stored[b], 16)

            with sp.Fori(0, NB // 2 - 1) as i:
                for b in range(2):
                    batch(2 * i + b, b)
            for b in range(2):
                batch(NB - 2 + b, b, more=False)
            for b in range(2):
                sp.wait_ge(stored[b], NB // 2 * 16)

        @block.gpsimd
        def _(pool):
            def score_products(t, b, g):
                for j in range(CU):
                    c = g * CU + j
                    k = (2 * t + g) * CU + j
                    pool.wait_ge(qkv_ready, t * C + c + 1)
                    need(pool, qk_summed, k - QK_RING + 1)
                    q = qkv[b][:, c, 0:E].rearrange("p (d h) -> p d h", d=D)
                    kk = qkv[b][:, c, E:2 * E].rearrange("p (d h) -> p d h", d=D)
                    nc.gpsimd.tensor_tensor(
                        qk_prod[c % QK_RING][:, :, :, :],
                        q.unsqueeze(3).to_broadcast([P, D, H, H]), kk.unsqueeze(2).to_broadcast([P, D, H, H]),
                        ALU.mult).then_inc(qk_prod_ready, 1)

            def value_products(t, b, g):
                v = 2 * t + g
                c = g * CU + CU - 1
                pool.wait_ge(prob_a, 2 * v + 1)
                need(pool, pv_summed, v)
                pr = prob_sb[g][:, :].rearrange("p (q k) -> p k q", q=H)
                val = qkv[b][:, c, 2 * E:3 * E].rearrange("p (k d) -> p k d", k=H)
                nc.gpsimd.tensor_tensor(
                    pv_pool[:, :, :, :],
                    pr.unsqueeze(3).to_broadcast([P, H, H, D]), val.unsqueeze(2).to_broadcast([P, H, H, D]),
                    ALU.mult).then_inc(pv_prod_ready, 1)

            def batch(t, b, more=True):
                score_products(t, b, 1)
                value_products(t, b, 0)
                if more:
                    score_products(t + 1, 1 - b, 0)
                value_products(t, b, 1)

            score_products(0, 0, 0)
            steps(pool, batch)

        @block.scalar
        def _(act):
            act.wait_ge(small_in, 48)
            nc.scalar.activation(sig[:, :], cT[:, :], ACT.Exp, scale=-1.0).then_inc(exp_c, 1)

            def prepare(t, b):
                act.wait_ge(var_ready, t + 1)
                nc.scalar.activation(std[:, :], var[:, :], ACT.Sqrt).then_inc(std_ready, 1)
                for r in range(2):
                    act.wait_ge(xt_mm, 2 * t + r + 1)
                    need(act, qkv_mm, t * C)
                    nc.scalar.activation(hT[:, r * 512:r * 512 + 512], t_acc, ACT.Identity,
                                         bias=shift[b][:, 0, :], scale=shift[b][:, 1, :]).then_inc(hT_done, 1)

            def probabilities(t, g):
                v = 2 * t + g
                act.wait_ge(less_v, v + 1)
                need(act, pv_prod_ready, v - 1)
                nc.scalar.activation(prob_sb[g][:, :], less[:, CU - 1, :], ACT.Exp, scale=SCALE).then_inc(prob_a, 1)
                nc.scalar.activation(score[g][:, 0:DVE_PV, :], less[:, 0:DVE_PV, :], ACT.Exp,
                                     scale=SCALE).then_inc(prob_a, 1)

            def batch(t, b, more=True):
                probabilities(t, 0)
                if more:
                    prepare(t + 1, 1 - b)
                probabilities(t, 1)

            act.wait_ge(mod_v, 6)
            prepare(0, 0)
            steps(act, batch)

        @block.vector
        def _(dve):
            dve.wait_ge(exp_c, 1)
            nc.vector.tensor_scalar(sig[:, :], sig[:, :], 1.0, None, ALU.add).then_inc(silu_v, 1)
            dve.wait_ge(silu_v, 1)
            nc.vector.reciprocal(sig[:, :], sig[:, :]).then_inc(silu_v, 1)
            dve.wait_ge(silu_v, 2)
            nc.vector.tensor_tensor(silu[:, :], cT[:, :], sig[:, :], ALU.mult).then_inc(silu_v, 1)
            dve.wait_ge(mod_mm, 1)
            nc.vector.tensor_copy(raw[:, :, :], t_acc[:, 0:6 * NB].rearrange("p (j n) -> p j n", j=6)).then_inc(silu_v, 1)
            dve.wait_ge(silu_v, 4)
            nc.vector.tensor_copy(mod[:, 0:6:3, :], raw[:, 0:6:3, :]).then_inc(mod_v, 1)
            nc.vector.tensor_scalar(mod[:, 1:6:3, :], raw[:, 1:6:3, :], 1.0, None, ALU.add).then_inc(mod_v, 1)
            nc.vector.tensor_scalar(sgn[:, :, :], raw[:, 2:6:3, :], 0.0, 2.0, ALU.is_ge, ALU.mult).then_inc(mod_v, 1)
            nc.vector.scalar_tensor_tensor(mag[:, :, :], raw[:, 2:6:3, :], -1.0, raw[:, 2:6:3, :],
                                           ALU.mult, ALU.max).then_inc(mod_v, 1)
            dve.wait_ge(mod_v, 4)
            nc.vector.tensor_scalar(mag[:, :, :], mag[:, :, :], 0.25, None, ALU.max).then_inc(mod_v, 1)
            dve.wait_ge(mod_v, 5)
            nc.vector.scalar_tensor_tensor(mod[:, 2:6:3, :], sgn[:, :, :], -1.0, mag[:, :, :],
                                           ALU.add, ALU.mult).then_inc(mod_v, 1)
            LN = C + 3

            def statistics(t, b, full):
                dve.wait_ge(x_in[b], full)
                for c in range(C):
                    nc.vector.bn_stats(stats[:, c, :], x[b][:, c, :]).then_inc(ln_v, 1)
                moments(nc, dve, stats, mean[:, :], tmp, var[:, :], ln_v, t * LN + C, var_ready)

            def normalise(t, b):
                nc.vector.tensor_copy(shift[b][:, :, :], mod[:, 0:2, bass.ds(t, 1)])
                dve.wait_ge(std_ready, t + 1)
                nc.vector.reciprocal(rstd[:, :], std[:, :]).then_inc(ln_v, 1)
                dve.wait_ge(ln_v, t * LN + LN)
                for c in range(C):
                    last = nc.vector.tensor_scalar(x[b][:, c, :], x[b][:, c, :], mean[:, c:c + 1],
                                                   rstd[:, c:c + 1], ALU.subtract, ALU.mult)
                last.then_inc(xn_ready, 1)

            def copy_qkv(t, b, cs):
                for c in cs:
                    k = t * C + c
                    dve.wait_ge(qkv_mm, k + 1)
                    need(dve, pv_prod_ready, 2 * t - 2)
                    nc.vector.tensor_tensor(qkv[b][:, c, :], q_acc[c % 2], bqkv[:, :], ALU.add).then_inc(qkv_ready, 1)

            def row_max(t, g):
                v = 2 * t + g
                dve.wait_ge(qk_summed, CU * v + CU)
                rows = score[g].rearrange("p c (q k) -> p (c q) k", q=H)
                nc.vector.tensor_reduce(top[:, :], rows, AX.X, ALU.max).then_inc(top_v, 1)
                dve.wait_ge(top_v, v + 1)
                nc.vector.tensor_tensor(less[:, :, :].rearrange("p c (q k) -> p (c q) k", q=H), rows,
                                        top[:, :].unsqueeze(2).to_broadcast([P, CU * H, H]),
                                        ALU.subtract).then_inc(less_v, 1)

            def row_sum(t, g):
                v = 2 * t + g
                dve.wait_ge(prob_a, 2 * v + 2)
                nc.vector.tensor_reduce(total[:, 0:DVE_PV * H],
                                        score[g][:, 0:DVE_PV, :].rearrange("p c (q k) -> p (c q) k", q=H),
                                        AX.X, ALU.add)
                nc.vector.tensor_reduce(total[:, DVE_PV * H:CU * H],
                                        prob_sb[g][:, :].rearrange("p (q k) -> p q k", q=H),
                                        AX.X, ALU.add).then_inc(total_v, 1)

            def values(t, b, g):
                v = 2 * t + g

                def product(j):
                    c = g * CU + j
                    pr = score[g][:, j, :].rearrange("p (q k) -> p q k", q=H)
                    val = qkv[b][:, c, 2 * E:3 * E].rearrange("p (k d) -> p d k", k=H)
                    nc.vector.tensor_tensor(pv_dve[j][:, :, :, :],
                                            pr.unsqueeze(2).to_broadcast([P, H, D, H]),
                                            val.unsqueeze(1).to_broadcast([P, H, D, H]),
                                            ALU.mult).then_inc(pv_mult_v, 1)

                def reduction(j):
                    dve.wait_ge(pv_mult_v, DVE_PV * v + j + 1)
                    nc.vector.tensor_reduce(sums[:, j, :].rearrange("p (q d) -> p q d", q=H), pv_dve[j][:, :, :, :],
                                            AX.X, ALU.add).then_inc(pv_sum_v, 1)

                product(0)
                for j in range(1, DVE_PV):
                    product(j)
                    reduction(j - 1)
                    if j == 1:
                        dve.wait_ge(total_v, v + 1)
                        nc.vector.reciprocal(recip[:, :], total[:, :]).then_inc(recip_v, 1)
                reduction(DVE_PV - 1)

            def divide(t, b, g, full):
                v = 2 * t + g
                need(dve, stored[b], full)
                dve.wait_ge(pv_sum_v, DVE_PV * v + DVE_PV)
                dve.wait_ge(recip_v, v + 1)
                r = recip[:, :].rearrange("p (c q) -> p c q", c=CU).unsqueeze(3).to_broadcast([P, CU, H, D])
                o = out[b][:, :, g * CU:g * CU + CU, :].rearrange("p q c d -> p c q d")
                nc.vector.tensor_tensor(o[:, 0:DVE_PV], sums[:, :, :].rearrange("p c (q d) -> p c q d", q=H),
                                        r[:, 0:DVE_PV], ALU.mult)
                dve.wait_ge(pv_summed, v + 1)
                nc.vector.tensor_tensor(o[:, DVE_PV], o_acc.rearrange("p (q d) -> p q d", q=H), r[:, DVE_PV],
                                        ALU.mult).then_inc(norm_v, 1)

            def batch(t, b, more=True, i=None):
                i = t // 2 if isinstance(t, int) else i
                row_max(t, 0)
                if more:
                    statistics(t + 1, 1 - b, 16 * (i + b) + 16)
                row_sum(t, 0)
                values(t, b, 0)
                if more:
                    normalise(t + 1, 1 - b)
                divide(t, b, 0, 16 * i)
                row_max(t, 1)
                if more:
                    copy_qkv(t + 1, 1 - b, range(CU))
                row_sum(t, 1)
                values(t, b, 1)
                if more:
                    copy_qkv(t + 1, 1 - b, range(CU, C))
                divide(t, b, 1, 16 * i)

            statistics(0, 0, 16)
            normalise(0, 0)
            copy_qkv(0, 0, range(C))
            for b in range(2):
                batch(b, b)
            with dve.Fori(1, NB // 2 - 1) as i:
                for b in range(2):
                    batch(2 * i + b, b, i=i)
            for b in range(2):
                batch(NB - 2 + b, b, more=b == 0)

        @block.tensor
        def _(pe):
            pe.wait_ge(wmod_in, 16)
            pe.wait_ge(silu_v, 3)
            for j in range(6):
                last = nc.tensor.matmul(t_acc[:, j * NB:j * NB + NB], wmod[:, j, :], silu[:, :], start=True, stop=True)
            last.then_inc(mod_mm, 1)
            pe.wait_ge(silu_v, 4)

            def turn(t, b):
                for r in range(2):
                    pe.wait_ge(xn_ready, t + 1)
                    need(pe, hT_done, 2 * t + r)
                    for j in range(CU):
                        last = nc.tensor.transpose(t_acc[:, j * P:j * P + P], x[b][:, r * CU + j, :], ident[:, :])
                    last.then_inc(xt_mm, 1)

            def project(t, cs):
                for c in cs:
                    k = t * C + c
                    if c % CU == 0:
                        pe.wait_ge(hT_done, 2 * t + c // CU + 1)
                    need(pe, qkv_ready, k - 1)
                    nc.tensor.matmul(q_acc[c % 2], hT[:, c * P:c * P + P], wqkv[:, :],
                                     start=True, stop=True).then_inc(qkv_mm, 1)

            def sum_scores(t, b, g):
                v = 2 * t + g
                need(pe, pv_mult_v, DVE_PV * (v - 1))
                for j in range(CU):
                    c = g * CU + j
                    pe.wait_ge(qk_prod_ready, CU * v + j + 1)
                    for d in range(D):
                        last = nc.tensor.matmul(score[g][:, j, :], ident[:, :],
                                                flat(qk_prod[c % QK_RING][:, d, :, :]), start=d == 0, stop=d == D - 1)
                    last.then_inc(qk_summed, 1)

            def sum_values(t, g):
                v = 2 * t + g
                pe.wait_ge(pv_prod_ready, v + 1)
                need(pe, norm_v, v)
                for k in range(H):
                    last = nc.tensor.matmul(o_acc, ident[:, :], flat(pv_pool[:, k, :, :]),
                                            start=k == 0, stop=k == H - 1)
                last.then_inc(pv_summed, 1)

            def batch(t, b, more=True):
                sum_scores(t, b, 1)
                if more:
                    turn(t + 1, 1 - b)
                sum_values(t, 0)
                if more:
                    project(t + 1, range(CU + 2))
                    sum_scores(t + 1, 1 - b, 0)
                    project(t + 1, range(CU + 2, C))
                sum_values(t, 1)

            turn(0, 0)
            project(0, range(C))
            sum_scores(0, 0, 0)
            steps(pe, batch)


def merge(nc, io, scr, mod, ident, logits, ps):
    with ExitStack() as ctx:
        sb = lambda n, s, d=F32: ctx.enter_context(nc.sbuf_tensor("merge_" + n, s, d))
        sem = lambda n: ctx.enter_context(nc.semaphore("merge_" + n))
        wo, bo, bog = sb("woT", [P, E]), sb("bo_col", [P, 1]), sb("bo_gate", [P, NB])
        gw = sb("gate_w", [P, NX])
        o = [sb(f"o{b}", [P, C, E]) for b in range(2)]
        x = [sb(f"x_in{b}", [P, C, E]) for b in range(2)]
        attn = sb("attnT", [P, S])
        proj, x1, xn = sb("projT", [P, S]), sb("x1", [P, C, E]), sb("xn", [P, C, E])
        now = [sb(f"now{b}", [P, 4, 1]) for b in range(2)]
        stats, mean, var = sb("stats", [P, C, 6]), sb("mean", [P, C]), sb("var", [P, C])
        tmp = [sb(f"moment_tmp{k}", [P, C])[:, :] for k in range(3)]
        std, rstd, h2 = sb("std", [P, C]), sb("rstd", [P, C]), sb("h2T", [P, S])
        w_in, gate_v = sem("w_in"), sem("bo_gated")
        o_in = [sem(f"o_in{b}") for b in range(2)]
        x_in = [sem(f"x_in{b}") for b in range(2)]
        o_tr, attn_v, proj_mm, proj_a, proj_tr = (
            sem("o_tr"), sem("attn_v"), sem("proj_mm"), sem("proj_a"), sem("proj_tr"))
        x1_v, ln_v, var_v, std_a, xn_v, xn_tr, h2_a = (
            sem("x1_v"), sem("ln_v"), sem("var_v"), sem("std_a"), sem("xn_v"), sem("xn_tr"), sem("h2_a"))
        logit_mm, logit_v = sem("logit_mm"), sem("logit_v")
        x1_st, h2_st = sem("x1_stored"), sem("h2_stored")
        pA, pB, pC, pD = (flat(ps[:, 2 * j:2 * j + 2, :]) for j in range(4))
        x_dram = io["x"].rearrange("n (p c) e -> n p c e", c=C)
        o_dram = scr["o"].rearrange("n h (r c e) -> n (h r) c e", c=C, e=E)
        block = ctx.enter_context(nc.Block())

        def steps(engine, batch):
            for b in range(2):
                batch(b, b, 0)
            with engine.Fori(1, NB // 2) as i:
                for b in range(2):
                    batch(2 * i + b, b, i)

        @block.sync
        def _(sp):
            sp.dma_start(wo[:, :], io["WoT"]).then_inc(w_in, 16)
            sp.dma_start(bo[:, :], io["bo"]).then_inc(w_in, 16)
            sp.dma_start(gw[:, :], io["gate_w"]).then_inc(w_in, 16)

            def load(n, b):
                sp.dma_start(o[b][:, :, :], o_dram[n]).then_inc(o_in[b], 16)
                sp.dma_start(x[b][:, :, :], x_dram[n]).then_inc(x_in[b], 16)

            def store(n):
                sp.wait_ge(x1_v, n + 1)
                sp.dma_start(scr["x1"][n], flat(x1[:, :, :])).then_inc(x1_st, 16)
                sp.wait_ge(h2_a, n + 1)
                sp.dma_start(scr["h2"][n], h2[:, :]).then_inc(h2_st, 16)

            for b in range(2):
                load(b, b)
            with sp.Fori(0, NB // 2 - 1) as i:
                for b in range(2):
                    store(2 * i + b)
                    load(2 * i + b + 2, b)
            for b in range(2):
                store(NB - 2 + b)
            sp.wait_ge(x1_st, 16 * NB)
            sp.wait_ge(h2_st, 16 * NB)

        @block.vector
        def _(dve):
            dve.wait_ge(w_in, 48)
            nc.vector.tensor_scalar(bog[:, :], mod[:, 2, :], bo[:, :], None, ALU.mult).then_inc(gate_v, 1)

            def batch(n, b, i):
                if b == 0 and isinstance(n, int):
                    dve.wait_ge(gate_v, 1)
                nc.vector.tensor_copy(now[b][:, 0:3, :], mod[:, 2:5, bass.ds(n, 1)])
                nc.vector.tensor_copy(now[b][:, 3, :], bog[:, bass.ds(n, 1)])
                dve.wait_ge(o_tr, n + 1)
                need(dve, proj_mm, n)
                nc.vector.tensor_copy(attn[:, :], pA).then_inc(attn_v, 1)
                dve.wait_ge(proj_tr, n + 1)
                dve.wait_ge(x_in[b], 16 * i + 16)
                need(dve, x1_st, 16 * n)
                nc.vector.tensor_tensor(flat(x1[:, :, :]), pC, flat(x[b][:, :, :]), ALU.add).then_inc(x1_v, 1)
                dve.wait_ge(x1_v, n + 1)
                base = n * (C + 3)
                for c in range(C):
                    nc.vector.bn_stats(stats[:, c, :], x1[:, c, :]).then_inc(ln_v, 1)
                moments(nc, dve, stats, mean[:, :], tmp, var[:, :], ln_v, base + C, var_v)
                dve.wait_ge(std_a, n + 1)
                nc.vector.reciprocal(rstd[:, :], std[:, :]).then_inc(ln_v, 1)
                dve.wait_ge(ln_v, base + C + 3)
                need(dve, xn_tr, n)
                for c in range(C):
                    last = nc.vector.tensor_scalar(xn[:, c, :], x1[:, c, :], mean[:, c:c + 1], rstd[:, c:c + 1],
                                                   ALU.subtract, ALU.mult)
                last.then_inc(xn_v, 1)
                dve.wait_ge(logit_mm, n + 1)
                nc.vector.tensor_copy(logits[:, bass.ds(n, 1), :, :].rearrange("p o c e -> p (o c e)"),
                                      pA[:, 0:C * NX]).then_inc(logit_v, 1)

            steps(dve, batch)

        @block.scalar
        def _(act):
            def batch(n, b, i):
                act.wait_ge(proj_mm, n + 1)
                need(act, proj_tr, n)
                nc.scalar.activation(proj[:, :], pB, ACT.Identity, bias=now[b][:, 3, :],
                                     scale=now[b][:, 0, :]).then_inc(proj_a, 1)
                act.wait_ge(var_v, n + 1)
                nc.scalar.activation(std[:, :], var[:, :], ACT.Sqrt).then_inc(std_a, 1)
                act.wait_ge(xn_tr, n + 1)
                need(act, h2_st, 16 * n)
                need(act, logit_mm, n)
                nc.scalar.activation(h2[:, :], pD, ACT.Identity, bias=now[b][:, 1, :],
                                     scale=now[b][:, 2, :]).then_inc(h2_a, 1)

            steps(act, batch)

        @block.tensor
        def _(pe):
            pe.wait_ge(w_in, 48)

            def batch(n, b, i):
                pe.wait_ge(o_in[b], 16 * i + 16)
                need(pe, logit_v, n)
                for c in range(C):
                    last = nc.tensor.transpose(pA[:, c * P:c * P + P], o[b][:, c, :], ident[:, :])
                last.then_inc(o_tr, 1)
                pe.wait_ge(attn_v, n + 1)
                need(pe, proj_a, n)
                for j in range(2):
                    last = nc.tensor.matmul(pB[:, j * 512:j * 512 + 512], wo[:, :],
                                            attn[:, j * 512:j * 512 + 512], start=True, stop=True)
                last.then_inc(proj_mm, 1)
                pe.wait_ge(proj_a, n + 1)
                need(pe, x1_v, n)
                for c in range(C):
                    last = nc.tensor.transpose(pC[:, c * P:c * P + P], proj[:, c * P:c * P + P], ident[:, :])
                last.then_inc(proj_tr, 1)
                pe.wait_ge(xn_v, n + 1)
                need(pe, h2_a, n)
                for c in range(C):
                    last = nc.tensor.transpose(pD[:, c * P:c * P + P], xn[:, c, :], ident[:, :])
                last.then_inc(xn_tr, 1)
                pe.wait_ge(h2_a, n + 1)
                for c in range(C):
                    last = nc.tensor.matmul(pA[:, c * NX:c * NX + NX], h2[:, c * P:c * P + P], gw[:, :],
                                            start=True, stop=True)
                last.then_inc(logit_mm, 1)

            steps(pe, batch)


def route(nc, io, scr, ident, logits, ps):
    T = NB * C
    with ExitStack() as ctx:
        sb = lambda n, s, d=F32: ctx.enter_context(nc.sbuf_tensor("route_" + n, s, d))
        sem = lambda n: ctx.enter_context(nc.semaphore("route_" + n))
        gb, rank = sb("gate_b_rows", [P, NX]), sb("rank_rows", [P, NX])
        lg = sb("lg", [P, T, NX])
        pick = [sb(f"pick{k}", [P, T, NX]) for k in range(2)]
        work = sb("work", [P, T, NX])
        top = [sb(f"top{k}", [P, T]) for k in range(2)]
        first = sb("first", [P, T])
        gap, weight = sb("gap", [P, T]), [sb(f"weight{k}", [P, T]) for k in range(2)]
        comb = sb("comb", [P, NB, NX, C])
        combT = sb("combT", [NX * C, NB, P])
        g_in, v, gap_v, exp_a, comb_v, comb_tr, combT_v, comb_st = (
            sem("gate_in"), sem("route_v"), sem("gap_v"), sem("gap_exp"), sem("comb_v"), sem("comb_tr"),
            sem("combT_v"), sem("comb_stored"))
        pT = flat(ps[0:NX * C, 0:2, :])
        block = ctx.enter_context(nc.Block())

        @block.sync
        def _(sp):
            sp.dma_start(gb[:, :], io["gate_b"].partition_broadcast(P)).then_inc(g_in, 16)
            sp.dma_start(rank[:, :], io["rank"].partition_broadcast(P)).then_inc(g_in, 16)
            sp.wait_ge(combT_v, 1)
            for e in range(NX):
                sp.dma_start(scr["comb"][e].rearrange("n c p -> c n p"),
                             combT[e * C:e * C + C, :, :]).then_inc(comb_st, 16)
            sp.wait_ge(comb_st, 16 * NX)

        @block.scalar
        def _(act):
            act.wait_ge(gap_v, 1)
            nc.scalar.activation(gap[:, :], gap[:, :], ACT.Exp).then_inc(exp_a, 1)

        @block.vector
        def _(dve):
            count = [0]

            def step(instruction):
                count[0] += 1
                instruction.then_inc(v, 1)
                dve.wait_ge(v, count[0])

            rows = lambda ap: ap.unsqueeze(1).to_broadcast([P, T, NX])
            cols = lambda ap: ap.unsqueeze(2).to_broadcast([P, T, NX])
            dve.wait_ge(g_in, 32)
            step(nc.vector.tensor_tensor(lg[:, :, :], logits[:, :, :, :].rearrange("p n c e -> p (n c) e"),
                                         rows(gb[:, :]), ALU.add))
            for k in range(2):
                step(nc.vector.tensor_reduce(top[k][:, :], lg[:, :, :], AX.X, ALU.max))
                step(nc.vector.tensor_tensor(work[:, :, :], lg[:, :, :], cols(top[k][:, :]), ALU.is_ge))
                step(nc.vector.tensor_tensor(work[:, :, :], work[:, :, :], rows(rank[:, :]), ALU.mult))
                step(nc.vector.tensor_reduce(first[:, :], work[:, :, :], AX.X, ALU.max))
                step(nc.vector.tensor_tensor(pick[k][:, :, :], work[:, :, :], cols(first[:, :]), ALU.is_equal))
                if k == 0:
                    step(nc.vector.scalar_tensor_tensor(lg[:, :, :], pick[0][:, :, :], -3.0e38, lg[:, :, :],
                                                        ALU.mult, ALU.add))
            nc.vector.tensor_tensor(gap[:, :], top[1][:, :], top[0][:, :], ALU.subtract).then_inc(gap_v, 1)
            dve.wait_ge(exp_a, 1)
            step(nc.vector.tensor_scalar(weight[0][:, :], gap[:, :], 1.0, None, ALU.add))
            step(nc.vector.reciprocal(weight[0][:, :], weight[0][:, :]))
            step(nc.vector.tensor_tensor(weight[1][:, :], weight[0][:, :], gap[:, :], ALU.mult))
            for k in range(2):
                step(nc.vector.tensor_tensor(pick[k][:, :, :], pick[k][:, :, :], cols(weight[k][:, :]), ALU.mult))
            nc.vector.tensor_tensor(comb[:, :, :, :].rearrange("p n e c -> p n c e"),
                                    pick[0][:, :, :].rearrange("p (n c) e -> p n c e", n=NB),
                                    pick[1][:, :, :].rearrange("p (n c) e -> p n c e", n=NB),
                                    ALU.add).then_inc(comb_v, 1)
            dve.wait_ge(comb_tr, 1)
            nc.vector.tensor_copy(combT[:, :, :].rearrange("x n p -> x (n p)"), pT).then_inc(combT_v, 1)

        @block.tensor
        def _(pe):
            pe.wait_ge(comb_v, 1)
            for n in range(NB):
                last = nc.tensor.transpose(pT[:, n * P:n * P + P],
                                           comb[:, n, :, :].rearrange("p e c -> p (e c)"), ident[:, :])
            last.then_inc(comb_tr, 1)


def feed(nc, io, scr, mod, ident, ps):
    NW = NX + 1
    with ExitStack() as ctx:
        sb = lambda n, s, d=F32: ctx.enter_context(nc.sbuf_tensor("feed_" + n, s, d))
        sem = lambda n: ctx.enter_context(nc.semaphore("feed_" + n))
        w1, w2 = sb("w1", [P, NW, HID]), sb("w2", [P, NW, HC, E])
        b1, b2 = sb("b1", [P, NW, HC]), sb("b2", [P, NW])
        h2 = [sb(f"h2_{b}", [P, BT]) for b in range(2)]
        wt = [sb(f"wt{b}", [P, NX, BT]) for b in range(2)]
        x1 = [sb(f"x1_{b}", [P, C // 2, E]) for b in range(2)]
        hid = [sb(f"hid{b}", [P, HC, BT]) for b in range(2)]
        part, acc = sb("weighted", [P, BT]), [sb(f"acc{b}", [P, BT]) for b in range(2)]
        y = [sb(f"y{b}", [P, C // 2, E]) for b in range(2)]
        w_in = sem("ffn_w_in")
        h2_in = [sem(f"h2_in{b}") for b in range(2)]
        wt_in = [sem(f"wt_in{b}") for b in range(2)]
        x1_in = [sem(f"x1_in{b}") for b in range(2)]
        up_mm, gelu_a, down_mm, down_v, acc_v, out_tr, y_v = (
            sem("up_mm"), sem("gelu_a"), sem("down_mm"), sem("down_read"), sem("acc_v"),
            sem("out_tr"), sem("y_v"))
        y_st = [sem(f"y_stored{b}") for b in range(2)]
        up = [ps[:, j, :] for j in range(HC)]
        down = [ps[:, 4 + j, :] for j in range(2)]
        tr = ps[:, 6, :]
        y_blocks = io["out"].rearrange("n (p b c) e -> n b p (c e)", b=2, c=C // 2)
        block = ctx.enter_context(nc.Block())
        PER = NW

        @block.sync
        def _(sp):
            sp.dma_start(w1[:, 0:NX, :], io["w1"].rearrange("e d h -> d e h")).then_inc(w_in, 16)
            sp.dma_start(w1[:, NX, :], io["ws1"]).then_inc(w_in, 16)
            for e in range(NX):
                sp.dma_start(w2[:, e, :, :], io["w2"][e].rearrange("(c p) d -> p c d", p=P)).then_inc(w_in, 16)
            sp.dma_start(w2[:, NX, :, :], io["ws2"].rearrange("(c p) d -> p c d", p=P)).then_inc(w_in, 16)
            sp.dma_start(b1[:, :, :].rearrange("p e c -> p (e c)"), io["b1T"]).then_inc(w_in, 16)
            sp.dma_start(b2[:, :], io["b2T"]).then_inc(w_in, 16)

            def load(n, b):
                cols = slice(b * BT, b * BT + BT)
                sp.dma_start(h2[b][:, :], scr["h2"][n][:, cols]).then_inc(h2_in[b], 16)
                sp.dma_start(wt[b][:, :, :], scr["comb"][:, n].rearrange("e c p -> e (c p)")[:, cols]
                             .partition_broadcast(P)).then_inc(wt_in[b], 16)
                sp.dma_start(flat(x1[b][:, :, :]), scr["x1"][n][:, cols]).then_inc(x1_in[b], 16)

            for b in range(2):
                load(0, b)
            def store(n, b):
                sp.wait_ge(y_v, 2 * n + b + 1)
                sp.dma_start(y_blocks[n, b], flat(y[b][:, :, :])).then_inc(y_st[b], 16)
            with sp.Fori(0, NB - 1) as n:
                for b in range(2):
                    store(n, b)
                    load(n + 1, b)
            for b in range(2):
                store(NB - 1, b)
            for b in range(2):
                sp.wait_ge(y_st[b], 16 * NB)

        @block.tensor
        def _(pe):
            def ups(n, b, e):
                for j in range(HC):
                    if not (isinstance(n, int) and n == 0 and b == 0 and e == 0):
                        pe.wait_ge(gelu_a, ((2 * n + b) * PER + e - 1) * HC + j + 1)
                    nc.tensor.matmul(up[j], w1[:, e, j * P:j * P + P], h2[b][:, :],
                                     start=True, stop=True).then_inc(up_mm, 1)

            def downs(n, b, e):
                k = (2 * n + b) * PER + e
                if not (isinstance(n, int) and n == 0 and b == 0 and e < 2):
                    pe.wait_ge(down_v, k - 1)
                for j in range(HC):
                    pe.wait_ge(gelu_a, k * HC + j + 1)
                    last = nc.tensor.matmul(down[(b * PER + e) % 2], w2[:, e, j, :], hid[(b * PER + e) % 2][:, j, :],
                                            start=j == 0, stop=j == HC - 1)
                last.then_inc(down_mm, 1)

            def turn(n, b):
                pe.wait_ge(acc_v, (2 * n + b) * NX + NX)
                pe.wait_ge(y_v, 2 * n + b)
                for c in range(C // 2):
                    last = nc.tensor.transpose(tr[:, c * P:c * P + P], acc[b][:, c * P:c * P + P], ident[:, :])
                last.then_inc(out_tr, 1)

            def batch(n, first=False):
                for b in range(2):
                    pe.wait_ge(h2_in[b], 16 * n + 16)
                    for e in range(PER):
                        ups(n, b, e)
                        if e > 0:
                            downs(n, b, e - 1)
                        elif b > 0:
                            downs(n, 0, PER - 1)
                        elif not first:
                            downs(n - 1, 1, PER - 1)
                        if e == 2:
                            if b > 0:
                                turn(n, 0)
                            elif not first:
                                turn(n - 1, 1)

            pe.wait_ge(w_in, 13 * 16)
            batch(0, first=True)
            with pe.Fori(1, NB) as n:
                batch(n)
            downs(NB - 1, 1, PER - 1)
            turn(NB - 1, 1)

        @block.scalar
        def _(act):
            act.wait_ge(w_in, 13 * 16)

            def batch(n, first=False):
                for b in range(2):
                    for e in range(PER):
                        k = (2 * n + b) * PER + e
                        if not (first and b == 0 and e < 2):
                            act.wait_ge(down_mm, k - 1)
                        for j in range(HC):
                            act.wait_ge(up_mm, k * HC + j + 1)
                            nc.scalar.activation(hid[(b * PER + e) % 2][:, j, :], up[j], ACT.Gelu,
                                                 bias=b1[:, e, j:j + 1]).then_inc(gelu_a, 1)

            batch(0, first=True)
            with act.Fori(1, NB) as n:
                batch(n)

        @block.vector
        def _(dve):
            dve.wait_ge(w_in, 13 * 16)

            def batch(n, first=False):
                for b in range(2):
                    dve.wait_ge(wt_in[b], 16 * n + 16)
                    if not first:
                        dve.wait_ge(out_tr, 2 * n + b - 1)
                    for e in range(PER):
                        k = (2 * n + b) * PER + e
                        dve.wait_ge(down_mm, k + 1)
                        p = down[(b * PER + e) % 2]
                        if e == 0:
                            nc.vector.scalar_tensor_tensor(acc[b][:, :], p, b2[:, e:e + 1], wt[b][:, e, :],
                                                           ALU.add, ALU.mult).then_inc(down_v, 1)
                        elif e < NX:
                            dve.wait_ge(acc_v, (2 * n + b) * NX + e - 1)
                            nc.vector.scalar_tensor_tensor(part[:, :], p, b2[:, e:e + 1], wt[b][:, e, :],
                                                           ALU.add, ALU.mult).then_inc(down_v, 1)
                            dve.wait_ge(down_v, k + 1)
                            nc.vector.tensor_tensor(acc[b][:, :], acc[b][:, :], part[:, :], ALU.add).then_inc(acc_v, 1)
                        else:
                            dve.wait_ge(acc_v, (2 * n + b) * NX + NX - 1)
                            nc.vector.scalar_tensor_tensor(acc[b][:, :], p, b2[:, e:e + 1], acc[b][:, :],
                                                           ALU.add, ALU.add).then_inc(down_v, 1)
                            dve.wait_ge(down_v, k + 1)
                            nc.vector.tensor_scalar(acc[b][:, :], acc[b][:, :], mod[:, 5, bass.ds(n, 1)], None,
                                                    ALU.mult).then_inc(acc_v, 1)
                        if e == 3:
                            if b > 0:
                                finish(n, 0, first)
                            elif not first:
                                finish(n - 1, 1, False)

            def finish(n, b, first):
                dve.wait_ge(out_tr, 2 * n + b + 1)
                dve.wait_ge(x1_in[b], 16 * n + 16)
                dve.wait_ge(y_st[b], 16 * n)
                nc.vector.tensor_tensor(flat(y[b][:, :, :]), tr, flat(x1[b][:, :, :]), ALU.add).then_inc(y_v, 1)

            batch(0, first=True)
            with dve.Fori(1, NB) as n:
                batch(n)
            finish(NB - 1, 1, False)


def block_kernel(nc, io, out):
    io = dict(io, out=out)
    with ExitStack() as ctx:
        ps = ctx.enter_context(nc.psum_tensor("ps", [P, 8, 512], F32))
        mod = ctx.enter_context(nc.sbuf_tensor("mod", [P, 6, NB], F32))
        ident = ctx.enter_context(nc.sbuf_tensor("ident", [P, P], F32))
        logits = ctx.enter_context(nc.sbuf_tensor("logits", [P, NB, C, NX], F32))
        ident_in = ctx.enter_context(nc.semaphore("ident_in"))
        scr = {
            "o": nc.dram_tensor("o_scratch", [NB, H, S * D], F32).ap(),
            "x1": nc.dram_tensor("x1_scratch", [NB, P, C * E], F32).ap(),
            "h2": nc.dram_tensor("h2_scratch", [NB, P, S], F32).ap(),
            "comb": nc.dram_tensor("comb_scratch", [NX, NB, C, P], F32).ap(),
        }
        with nc.Block() as block:
            @block.sync
            def _(sp):
                sp.dma_start(ident[:, :], io["ident"]).then_inc(ident_in, 16)
                sp.wait_ge(ident_in, 16)
        attend(nc, io, scr, mod, ident, ps)
        merge(nc, io, scr, mod, ident, logits, ps)
        route(nc, io, scr, ident, logits, ps)
        feed(nc, io, scr, mod, ident, ps)


def kernel(**inputs):
    import numpy as np
    import concourse.bacc as bacc
    from concourse.bass_utils import run_bass_kernel_spmd

    a = {k[3:]: np.asarray(v) for k, v in inputs.items()}
    order = np.arange(E).reshape(H, D).T.reshape(-1)
    b1 = np.concatenate([a["ffn_b1"], a["ffn_bs1"][None]])
    b2 = np.concatenate([a["ffn_b2"], a["ffn_bs2"][None]])
    arrays = {
        "x": a["attn_x"], "cT": a["c"].T, "wmod": a["wmod"], "ident": np.eye(P, dtype=np.float32),
        "w_qkv": np.concatenate([a["attn_Wq"].T[:, order], a["attn_Wk"].T[:, order], a["attn_Wv"].T], 1),
        "b_qkv": np.concatenate([a["attn_bq"][order], a["attn_bk"][order], a["attn_bv"]]),
        "WoT": a["attn_Wo"].T, "bo": a["attn_bo"][:, None], "gate_w": a["ffn_gate_w"],
        "gate_b": a["ffn_gate_b"], "rank": np.arange(NX, 0, -1).astype(np.float32),
        "w1": a["ffn_w1"], "w2": a["ffn_w2"], "ws1": a["ffn_ws1"], "ws2": a["ffn_ws2"],
        "b1T": b1.reshape(NX + 1, HC, P).transpose(2, 0, 1).reshape(P, -1), "b2T": b2.T,
    }
    arrays = {k: np.ascontiguousarray(v) for k, v in arrays.items()}
    nc = bacc.Bacc("TRN2", target_bir_lowering=False, num_devices=1)
    io = {k: nc.dram_tensor(f"in_{k}", v.shape, mybir.dt.from_np(v.dtype), kind="ExternalInput").ap()
          for k, v in arrays.items()}
    out = nc.dram_tensor("out", (NB, S, E), F32, kind="ExternalOutput").ap()
    block_kernel(nc, io, out)
    r = run_bass_kernel_spmd(nc, [{f"in_{k}": v for k, v in arrays.items()}], core_ids=[0])
    return r.results[0]["out"]
```

```python
from contextlib import ExitStack

import concourse.bass as bass
from concourse import mybir

F32, I32 = mybir.dt.float32, mybir.dt.int32
ALU = mybir.AluOpType
ACT = mybir.ActivationFunctionType
AX = mybir.AxisListType

NB, S, E = 8, 1024, 128
P = 128
H, D = 16, 8
HH = H * H
C = S // P
CU = C // 2
SCALE = 1.0 / D ** 0.5
EPS = 1e-5
NX, HID = 8, 512
HC = HID // P
BT = 512
BLOCKS = 2 * NB * S // BT + NX - 1


def flat(ap):
    return ap.rearrange("p a b -> p (a b)")


def need(engine, semaphore, count):
    if not isinstance(count, int) or count > 0:
        engine.wait_ge(semaphore, count)


def moments(nc, dve, stats, mean, tmp, var, ln_v, base, ready):
    total, gap, squares = tmp
    dve.wait_ge(ln_v, base)
    nc.vector.tensor_tensor(total, stats[:, :, 1], stats[:, :, 4], ALU.add)
    nc.vector.tensor_tensor(gap, stats[:, :, 1], stats[:, :, 4], ALU.subtract)
    nc.vector.tensor_tensor(squares, stats[:, :, 2], stats[:, :, 5], ALU.add).then_inc(ln_v, 1)
    dve.wait_ge(ln_v, base + 1)
    nc.vector.tensor_scalar(mean, total, 0.5, None, ALU.mult)
    nc.vector.scalar_tensor_tensor(gap, gap, 0.25, gap, ALU.mult, ALU.mult)
    nc.vector.tensor_scalar(squares, squares, 1.0 / E, EPS, ALU.mult, ALU.add).then_inc(ln_v, 1)
    dve.wait_ge(ln_v, base + 2)
    nc.vector.tensor_tensor(var, gap, squares, ALU.add).then_inc(ready, 1)


def attend(nc, io, scr, mod, ident, silu, ps):
    with ExitStack() as ctx:
        sb = lambda n, s, d=F32: ctx.enter_context(nc.sbuf_tensor("attend_" + n, s, d))
        sem = lambda n: ctx.enter_context(nc.semaphore("attend_" + n))
        cT, sig = sb("cT", [P, NB]), sb("sig", [P, NB])
        zeros, zeros_p, zeroed = sb("zeros", [P, BLOCKS, E + 2]), sem("zeros_p"), sem("slots_zeroed")
        wmod, raw = sb("wmod", [P, 6, E]), sb("raw_mod", [P, 6, NB])
        sgn, mag = sb("sgn", [P, 2, NB]), sb("mag", [P, 2, NB])
        wqkv, bqkv = sb("w_qkv", [P, 3 * E]), sb("b_qkv", [P, 3 * E])
        x = [sb(f"x{b}", [P, C, E]) for b in range(2)]
        stats, mean = sb("stats", [P, C, 6]), sb("mean", [P, C])
        tmp = [sb(f"moment_tmp{k}", [P, C])[:, :] for k in range(3)]
        var, std, rstd = sb("var", [P, C]), sb("std", [P, C]), sb("rstd", [P, C])
        shift = [sb(f"shift{b}", [P, 2, 1]) for b in range(2)]
        hT = sb("hT", [P, S])
        qkv = [sb(f"qkv{b}", [P, C, 3 * E]) for b in range(2)]
        QK_RING = CU
        qk_prod = [sb(f"qk_prod{r}", [P, D, H, H]) for r in range(QK_RING)]
        pv_pool = sb("pv_prod_pool", [P, H, H, D])
        DVE_PV = CU - 1
        pv_dve = [sb(f"pv_prod_dve{r}", [P, H, D, H]) for r in range(DVE_PV)]
        top, less = sb("row_max", [P, CU * H]), sb("less_max", [P, CU, HH])
        prob_sb = [sb(f"prob_last{g}", [P, HH]) for g in range(2)]
        total, recip = sb("row_sum", [P, CU * H]), sb("row_recip", [P, CU * H])
        sums = sb("sums", [P, DVE_PV, E])
        out = [sb(f"out{b}", [P, H, C, D]) for b in range(2)]

        small_in, wmod_in, exp_c, silu_v = sem("small_in"), sem("wmod_in"), sem("exp_neg_c"), sem("silu_v")
        mod_mm, mod_v = sem("mod_mm"), sem("mod_v")
        x_in = [sem(f"x_in{b}") for b in range(2)]
        ln_v, var_ready, std_ready = sem("ln_v"), sem("var_ready"), sem("std_ready")
        xn_ready, xt_mm, hT_done = sem("xn_ready"), sem("xt_mm"), sem("hT_done")
        qkv_mm, qkv_ready = sem("qkv_mm"), sem("qkv_ready")
        qk_prod_ready, qk_summed = sem("qk_prod_ready"), sem("qk_summed")
        top_v, less_v, prob_a, total_v, recip_v = (
            sem("row_max_v"), sem("less_max_v"), sem("prob_a"), sem("row_sum_v"), sem("row_recip_v"))
        pv_prod_ready, pv_summed = sem("pv_prod_ready"), sem("pv_summed")
        pv_mult_v, pv_sum_v, norm_v = sem("pv_mult_v"), sem("pv_sum_v"), sem("norm_v")
        stored = [sem(f"out_stored{b}") for b in range(2)]

        score = [ps[:, 2 * g:2 * g + 2, :].rearrange("p a (b s) -> p (a b) s", b=2) for g in range(2)]
        q_acc = [ps[:, 4 + j, 0:3 * E] for j in range(2)]
        t_acc, o_acc = ps[:, 6, :], ps[:, 7, 0:E]
        x_dram = io["x"].rearrange("n (p c) e -> n p c e", c=C)
        o_dram = scr["o"].rearrange("n h (p x) -> n p h x", p=P)
        block = ctx.enter_context(nc.Block())

        def steps(engine, batch):
            for b in range(2):
                batch(b, b)
            with engine.Fori(1, NB // 2 - 1) as i:
                for b in range(2):
                    batch(2 * i + b, b)
            for b in range(2):
                batch(NB - 2 + b, b, more=b == 0)

        @block.sync
        def _(sp):
            for dst, name in ((cT, "cT"), (wqkv, "w_qkv")):
                sp.dma_start(dst[:, :], io[name]).then_inc(small_in, 16)
            sp.dma_start(x[0][:, :, :], x_dram[0]).then_inc(x_in[0], 16)
            sp.dma_start(flat(wmod[:, :, :]), io["wmod"]).then_inc(wmod_in, 16)
            sp.dma_start(bqkv[:, :], io["b_qkv"].partition_broadcast(P)).then_inc(small_in, 16)
            sp.dma_start(x[1][:, :, :], x_dram[1]).then_inc(x_in[1], 16)
            sp.wait_ge(zeros_p, 1)
            slots = scr["slots"].rearrange("(q m p) e -> q p m e", q=BT // P, p=P)
            for q in range(BT // P):
                sp.dma_start(slots[q], zeros[:, :, :]).then_inc(zeroed, 16)

            def batch(t, b, more=True):
                if more:
                    sp.wait_ge(xt_mm, 2 * t + 2)
                    sp.dma_start(x[b][:, :, :], x_dram[t + 2]).then_inc(x_in[b], 16)
                sp.wait_ge(norm_v, 2 * t + 2)
                sp.dma_start(o_dram[t], out[b][:, :, :, :].rearrange("p h c d -> p h (c d)")).then_inc(stored[b], 16)

            with sp.Fori(0, NB // 2 - 1) as i:
                for b in range(2):
                    batch(2 * i + b, b)
            for b in range(2):
                batch(NB - 2 + b, b, more=False)
            for b in range(2):
                sp.wait_ge(stored[b], NB // 2 * 16)
            sp.wait_ge(zeroed, BT // P * 16)

        @block.gpsimd
        def _(pool):
            def score_products(t, b, g):
                for j in range(CU):
                    c = g * CU + j
                    k = (2 * t + g) * CU + j
                    pool.wait_ge(qkv_ready, t * C + c + 1)
                    need(pool, qk_summed, k - QK_RING + 1)
                    q = qkv[b][:, c, 0:E].rearrange("p (d h) -> p d h", d=D)
                    kk = qkv[b][:, c, E:2 * E].rearrange("p (d h) -> p d h", d=D)
                    nc.gpsimd.tensor_tensor(
                        qk_prod[c % QK_RING][:, :, :, :],
                        q.unsqueeze(3).to_broadcast([P, D, H, H]), kk.unsqueeze(2).to_broadcast([P, D, H, H]),
                        ALU.mult).then_inc(qk_prod_ready, 1)

            def value_products(t, b, g):
                v = 2 * t + g
                c = g * CU + CU - 1
                pool.wait_ge(prob_a, 2 * v + 1)
                need(pool, pv_summed, v)
                pr = prob_sb[g][:, :].rearrange("p (q k) -> p k q", q=H)
                val = qkv[b][:, c, 2 * E:3 * E].rearrange("p (k d) -> p k d", k=H)
                nc.gpsimd.tensor_tensor(
                    pv_pool[:, :, :, :],
                    pr.unsqueeze(3).to_broadcast([P, H, H, D]), val.unsqueeze(2).to_broadcast([P, H, H, D]),
                    ALU.mult).then_inc(pv_prod_ready, 1)

            def batch(t, b, more=True):
                score_products(t, b, 1)
                value_products(t, b, 0)
                if more:
                    score_products(t + 1, 1 - b, 0)
                value_products(t, b, 1)

            nc.gpsimd.memset(zeros[:, :, :], 0.0).then_inc(zeros_p, 1)
            score_products(0, 0, 0)
            steps(pool, batch)

        @block.scalar
        def _(act):
            act.wait_ge(small_in, 48)
            nc.scalar.activation(sig[:, :], cT[:, :], ACT.Exp, scale=-1.0).then_inc(exp_c, 1)

            def deviation(t):
                act.wait_ge(var_ready, t + 1)
                nc.scalar.activation(std[:, :], var[:, :], ACT.Sqrt).then_inc(std_ready, 1)

            def modulate(t, b):
                for r in range(2):
                    act.wait_ge(xt_mm, 2 * t + r + 1)
                    need(act, qkv_mm, t * C)
                    nc.scalar.activation(hT[:, r * 512:r * 512 + 512], t_acc, ACT.Identity,
                                         bias=shift[b][:, 0, :], scale=shift[b][:, 1, :]).then_inc(hT_done, 1)

            def probabilities(t, g):
                v = 2 * t + g
                act.wait_ge(less_v, v + 1)
                need(act, pv_prod_ready, v - 1)
                nc.scalar.activation(prob_sb[g][:, :], less[:, CU - 1, :], ACT.Exp, scale=SCALE).then_inc(prob_a, 1)
                nc.scalar.activation(score[g][:, 0:DVE_PV, :], less[:, 0:DVE_PV, :], ACT.Exp,
                                     scale=SCALE).then_inc(prob_a, 1)

            def batch(t, b, more=True, far=True):
                probabilities(t, 0)
                if more:
                    modulate(t + 1, 1 - b)
                probabilities(t, 1)
                if far:
                    deviation(t + 2)

            act.wait_ge(mod_v, 6)
            deviation(0)
            modulate(0, 0)
            deviation(1)
            for b in range(2):
                batch(b, b)
            with act.Fori(1, NB // 2 - 1) as i:
                for b in range(2):
                    batch(2 * i + b, b)
            for b in range(2):
                batch(NB - 2 + b, b, more=b == 0, far=False)

        @block.vector
        def _(dve):
            dve.wait_ge(exp_c, 1)
            nc.vector.tensor_scalar(sig[:, :], sig[:, :], 1.0, None, ALU.add).then_inc(silu_v, 1)
            dve.wait_ge(silu_v, 1)
            nc.vector.reciprocal(sig[:, :], sig[:, :]).then_inc(silu_v, 1)
            dve.wait_ge(silu_v, 2)
            nc.vector.tensor_tensor(silu[:, :], cT[:, :], sig[:, :], ALU.mult).then_inc(silu_v, 1)
            dve.wait_ge(mod_mm, 1)
            nc.vector.tensor_copy(raw[:, :, :], t_acc[:, 0:6 * NB].rearrange("p (j n) -> p j n", j=6)).then_inc(silu_v, 1)
            dve.wait_ge(silu_v, 4)
            nc.vector.tensor_copy(mod[:, 0:6:3, :], raw[:, 0:6:3, :]).then_inc(mod_v, 1)
            nc.vector.tensor_scalar(mod[:, 1:6:3, :], raw[:, 1:6:3, :], 1.0, None, ALU.add).then_inc(mod_v, 1)
            nc.vector.tensor_scalar(sgn[:, :, :], raw[:, 2:6:3, :], 0.0, 2.0, ALU.is_ge, ALU.mult).then_inc(mod_v, 1)
            nc.vector.scalar_tensor_tensor(mag[:, :, :], raw[:, 2:6:3, :], -1.0, raw[:, 2:6:3, :],
                                           ALU.mult, ALU.max).then_inc(mod_v, 1)
            dve.wait_ge(mod_v, 4)
            nc.vector.tensor_scalar(mag[:, :, :], mag[:, :, :], 0.25, None, ALU.max).then_inc(mod_v, 1)
            dve.wait_ge(mod_v, 5)
            nc.vector.scalar_tensor_tensor(mod[:, 2:6:3, :], sgn[:, :, :], -1.0, mag[:, :, :],
                                           ALU.add, ALU.mult).then_inc(mod_v, 1)
            LN = C + 3

            def statistics(t, b, full):
                dve.wait_ge(x_in[b], full)
                for c in range(C):
                    nc.vector.bn_stats(stats[:, c, :], x[b][:, c, :]).then_inc(ln_v, 1)
                moments(nc, dve, stats, mean[:, :], tmp, var[:, :], ln_v, t * LN + C, var_ready)

            def normalise(t, b):
                nc.vector.tensor_copy(shift[b][:, :, :], mod[:, 0:2, bass.ds(t, 1)])
                dve.wait_ge(std_ready, t + 1)
                nc.vector.reciprocal(rstd[:, :], std[:, :]).then_inc(ln_v, 1)
                dve.wait_ge(ln_v, t * LN + LN)
                for c in range(C):
                    last = nc.vector.tensor_scalar(x[b][:, c, :], x[b][:, c, :], mean[:, c:c + 1],
                                                   rstd[:, c:c + 1], ALU.subtract, ALU.mult)
                last.then_inc(xn_ready, 1)

            def copy_qkv(t, b, cs):
                for c in cs:
                    k = t * C + c
                    dve.wait_ge(qkv_mm, k + 1)
                    need(dve, pv_prod_ready, 2 * t - 2)
                    nc.vector.tensor_tensor(qkv[b][:, c, :], q_acc[c % 2], bqkv[:, :], ALU.add).then_inc(qkv_ready, 1)

            def row_max(t, g):
                v = 2 * t + g
                dve.wait_ge(qk_summed, CU * v + CU)
                rows = score[g].rearrange("p c (q k) -> p (c q) k", q=H)
                nc.vector.tensor_reduce(top[:, :], rows, AX.X, ALU.max).then_inc(top_v, 1)
                dve.wait_ge(top_v, v + 1)
                nc.vector.tensor_tensor(less[:, :, :].rearrange("p c (q k) -> p (c q) k", q=H), rows,
                                        top[:, :].unsqueeze(2).to_broadcast([P, CU * H, H]),
                                        ALU.subtract).then_inc(less_v, 1)

            def row_sum(t, g):
                v = 2 * t + g
                dve.wait_ge(prob_a, 2 * v + 2)
                nc.vector.tensor_reduce(total[:, 0:DVE_PV * H],
                                        score[g][:, 0:DVE_PV, :].rearrange("p c (q k) -> p (c q) k", q=H),
                                        AX.X, ALU.add)
                nc.vector.tensor_reduce(total[:, DVE_PV * H:CU * H],
                                        prob_sb[g][:, :].rearrange("p (q k) -> p q k", q=H),
                                        AX.X, ALU.add).then_inc(total_v, 1)

            def values(t, b, g, between):
                v = 2 * t + g

                def product(j):
                    c = g * CU + j
                    pr = score[g][:, j, :].rearrange("p (q k) -> p q k", q=H)
                    val = qkv[b][:, c, 2 * E:3 * E].rearrange("p (k d) -> p d k", k=H)
                    nc.vector.tensor_tensor(pv_dve[j][:, :, :, :],
                                            pr.unsqueeze(2).to_broadcast([P, H, D, H]),
                                            val.unsqueeze(1).to_broadcast([P, H, D, H]),
                                            ALU.mult).then_inc(pv_mult_v, 1)

                def reduction(j):
                    dve.wait_ge(pv_mult_v, DVE_PV * v + j + 1)
                    nc.vector.tensor_reduce(sums[:, j, :].rearrange("p (q d) -> p q d", q=H), pv_dve[j][:, :, :, :],
                                            AX.X, ALU.add).then_inc(pv_sum_v, 1)

                product(0)
                for j in range(1, DVE_PV):
                    product(j)
                    reduction(j - 1)
                    if j == 1:
                        dve.wait_ge(total_v, v + 1)
                        nc.vector.reciprocal(recip[:, :], total[:, :]).then_inc(recip_v, 1)
                between()
                reduction(DVE_PV - 1)

            def divide(t, b, g, full):
                v = 2 * t + g
                need(dve, stored[b], full)
                dve.wait_ge(pv_sum_v, DVE_PV * v + DVE_PV)
                dve.wait_ge(recip_v, v + 1)
                r = recip[:, :].rearrange("p (c q) -> p c q", c=CU).unsqueeze(3).to_broadcast([P, CU, H, D])
                o = out[b][:, :, g * CU:g * CU + CU, :].rearrange("p q c d -> p c q d")
                nc.vector.tensor_tensor(o[:, 0:DVE_PV], sums[:, :, :].rearrange("p c (q d) -> p c q d", q=H),
                                        r[:, 0:DVE_PV], ALU.mult)
                dve.wait_ge(pv_summed, v + 1)
                nc.vector.tensor_tensor(o[:, DVE_PV], o_acc.rearrange("p (q d) -> p q d", q=H), r[:, DVE_PV],
                                        ALU.mult).then_inc(norm_v, 1)

            def batch(t, b, more=True, far=True, i=None):
                i = t // 2 if isinstance(t, int) else i
                row_max(t, 0)
                if more:
                    normalise(t + 1, 1 - b)
                if isinstance(t, int) and t == 0:
                    pass
                elif b == 1:
                    divide(t - 1, 0, 1, 16 * i)
                else:
                    divide(t - 1, 1, 1, 16 * i - 16)
                row_sum(t, 0)
                values(t, b, 0, lambda: copy_qkv(t + 1, 1 - b, range(2)) if more else None)
                row_max(t, 1)
                if more:
                    copy_qkv(t + 1, 1 - b, range(2, CU + 1))
                if far:
                    statistics(t + 2, b, 16 * i + 32)
                divide(t, b, 0, 16 * i)
                row_sum(t, 1)
                values(t, b, 1, lambda: copy_qkv(t + 1, 1 - b, range(CU + 1, CU + 3)) if more else None)
                if more:
                    copy_qkv(t + 1, 1 - b, range(CU + 3, C))

            statistics(0, 0, 16)
            normalise(0, 0)
            copy_qkv(0, 0, range(C))
            statistics(1, 1, 16)
            for b in range(2):
                batch(b, b)
            with dve.Fori(1, NB // 2 - 1) as i:
                for b in range(2):
                    batch(2 * i + b, b, i=i)
            for b in range(2):
                batch(NB - 2 + b, b, more=b == 0, far=False)
            divide(NB - 1, 1, 1, NB // 2 * 16 - 16)

        @block.tensor
        def _(pe):
            pe.wait_ge(wmod_in, 16)
            pe.wait_ge(silu_v, 3)
            for j in range(6):
                last = nc.tensor.matmul(t_acc[:, j * NB:j * NB + NB], wmod[:, j, :], silu[:, :], start=True, stop=True)
            last.then_inc(mod_mm, 1)
            pe.wait_ge(silu_v, 4)

            def turn(t, b):
                for r in range(2):
                    pe.wait_ge(xn_ready, t + 1)
                    need(pe, hT_done, 2 * t + r)
                    for j in range(CU):
                        last = nc.tensor.transpose(t_acc[:, j * P:j * P + P], x[b][:, r * CU + j, :], ident[:, :])
                    last.then_inc(xt_mm, 1)

            def project(t, cs):
                for c in cs:
                    k = t * C + c
                    if c % CU == 0:
                        pe.wait_ge(hT_done, 2 * t + c // CU + 1)
                    need(pe, qkv_ready, k - 1)
                    nc.tensor.matmul(q_acc[c % 2], hT[:, c * P:c * P + P], wqkv[:, :],
                                     start=True, stop=True).then_inc(qkv_mm, 1)

            def sum_scores(t, b, g, js):
                v = 2 * t + g
                need(pe, pv_mult_v, DVE_PV * (v - 1))
                for j in js:
                    c = g * CU + j
                    pe.wait_ge(qk_prod_ready, CU * v + j + 1)
                    for d in range(D):
                        last = nc.tensor.matmul(score[g][:, j, :], ident[:, :],
                                                flat(qk_prod[c % QK_RING][:, d, :, :]), start=d == 0, stop=d == D - 1)
                    last.then_inc(qk_summed, 1)

            def sum_values(t, g):
                v = 2 * t + g
                pe.wait_ge(pv_prod_ready, v + 1)
                need(pe, norm_v, v)
                for k in range(H):
                    last = nc.tensor.matmul(o_acc, ident[:, :], flat(pv_pool[:, k, :, :]),
                                            start=k == 0, stop=k == H - 1)
                last.then_inc(pv_summed, 1)

            def batch(t, b, more=True):
                if more:
                    turn(t + 1, 1 - b)
                sum_scores(t, b, 1, range(2))
                if more:
                    project(t + 1, range(2))
                sum_scores(t, b, 1, range(2, CU))
                sum_values(t, 0)
                if more:
                    project(t + 1, range(2, CU + 1))
                    for j in range(CU):
                        sum_scores(t + 1, 1 - b, 0, range(j, j + 1))
                        if j != 2:
                            k = CU + 1 + j - (j > 2)
                            project(t + 1, range(k, k + 1))
                sum_values(t, 1)

            turn(0, 0)
            project(0, range(C))
            sum_scores(0, 0, 0, range(CU))
            steps(pe, batch)


def merge(nc, io, scr, keep, mod, ident, ps):
    x1, h2T, h2_rows, rows, logits, silu = (keep[k] for k in ("x1", "h2T", "h2_rows", "rows", "logits", "silu"))
    with ExitStack() as ctx:
        sb = lambda n, s, d=F32: ctx.enter_context(nc.sbuf_tensor("merge_" + n, s, d))
        sem = lambda n: ctx.enter_context(nc.semaphore("merge_" + n))
        wo, gw, bo = sb("woT", [P, E]), sb("gate_w", [P, NX]), sb("bo_rows", [P, E])
        wmod, silus = sb("wmod", [P, 4 * E]), sb("silu_wide", [P, NB, P])
        sign, size = sb("sign", [P, NB, E]), sb("size", [P, NB, E])
        bog = sb("bo_gated", [P, NB, E])
        wog = sb("wo_gated", [P, NB, E])
        o = [sb(f"o{b}", [P, C, E]) for b in range(2)]
        x = [sb(f"x_in{b}", [P, C, E]) for b in range(2)]
        xb = [sb(f"x_biased{b}", [P, C, E]) for b in range(2)]
        attn, xn = sb("attnT", [P, S]), [sb(f"xn{b}", [P, C, E]) for b in range(2)]
        h2 = [sb(f"h2T{b}", [P, S]) for b in range(2)]
        scaled = sb("scaled", [P, C, E])
        now = [sb(f"now{b}", [P, 2, 1]) for b in range(2)]
        stats, mean, var = sb("stats", [P, C, 6]), sb("mean", [P, C]), sb("var", [P, C])
        tmp = [sb(f"moment_tmp{k}", [P, C])[:, :] for k in range(3)]
        std, rstd = sb("std", [P, C]), sb("rstd", [P, C])
        w_in, wide_v, rows_mm, rows_v, bog_v = sem("w_in"), sem("wide_v"), sem("rows_mm"), sem("rows_v"), sem("bog_v")
        o_in = [sem(f"o_in{b}") for b in range(2)]
        x_in = [sem(f"x_in{b}") for b in range(2)]
        o_tr, attn_a, wog_v, xb_p, proj_mm = sem("o_tr"), sem("attn_a"), sem("wog_v"), sem("x_biased_p"), sem("proj_mm")
        x1_v, ln_v, var_v, std_a, xn_v, xn_tr, h2_a = (
            sem("x1_v"), sem("ln_v"), sem("var_v"), sem("std_a"), sem("xn_v"), sem("xn_tr"), sem("h2_a"))
        scaled_p, h2_rows_p = sem("scaled_p"), sem("h2_rows_p")
        logit_mm, logit_v = sem("logit_mm"), sem("logit_v")
        h2_kept = [sem(f"h2_kept{b}") for b in range(2)]
        pA, pB, pC = (flat(ps[:, 2 * j:2 * j + 2, :]) for j in range(3))
        pD = ps[:, 6, 0:C * NX]
        x_dram = io["x"].rearrange("n (p c) e -> n p c e", c=C)
        o_dram = scr["o"].rearrange("n h (r c e) -> n (h r) c e", c=C, e=E)
        block = ctx.enter_context(nc.Block())

        def steps(engine, first, second):
            def one(n, b, i, before):
                first(n, b, i)
                if before:
                    second(*before)

            one(0, 0, 0, None)
            one(1, 1, 0, (0, 0, 0))
            with engine.Fori(1, NB // 2) as i:
                one(2 * i, 0, i, (2 * i - 1, 1, i - 1))
                one(2 * i + 1, 1, i, (2 * i, 0, i))
            second(NB - 1, 1, NB // 2 - 1)

        def steps_ahead(engine, first, ahead, second, last=None):
            def one(n, b, i, before, after):
                if first:
                    first(n, b)
                if after:
                    ahead(*after)
                if before:
                    second(*before)
                if last:
                    last(n)

            ahead(0, 0, 0)
            one(0, 0, 0, None, (1, 1, 0))
            one(1, 1, 0, (0, 0, 0), (2, 0, 1))
            with engine.Fori(1, NB // 2 - 1) as i:
                one(2 * i, 0, i, (2 * i - 1, 1, i - 1), (2 * i + 1, 1, i))
                one(2 * i + 1, 1, i, (2 * i, 0, i), (2 * i + 2, 0, i + 1))
            i = NB // 2 - 1
            one(2 * i, 0, i, (2 * i - 1, 1, i - 1), (2 * i + 1, 1, i))
            one(2 * i + 1, 1, i, (2 * i, 0, i), None)
            second(NB - 1, 1, i)

        @block.sync
        def _(sp):
            sp.dma_start(wmod[:, :], io["wmod"][:, 2 * E:6 * E]).then_inc(w_in, 16)
            sp.dma_start(wo[:, :], io["WoT"]).then_inc(w_in, 16)
            sp.dma_start(bo[:, :], io["bo"].partition_broadcast(P)).then_inc(w_in, 16)
            sp.dma_start(gw[:, :], io["gate_w"]).then_inc(w_in, 16)

            def load(n, b):
                sp.dma_start(o[b][:, :, :], o_dram[n]).then_inc(o_in[b], 16)
                sp.dma_start(x[b][:, :, :], x_dram[n]).then_inc(x_in[b], 16)

            def store(n, b):
                sp.wait_ge(h2_a, n + 1)
                sp.dma_start(h2T[:, bass.ds(n, 1), :].rearrange("p o s -> p (o s)"), h2[b][:, :]).then_inc(h2_kept[b], 16)

            for b in range(2):
                load(b, b)
            with sp.Fori(0, NB // 2 - 1) as i:
                for b in range(2):
                    n = 2 * i + b
                    sp.wait_ge(x1_v, n + 1)
                    load(n + 2, b)
                    store(n, b)
            for b in range(2):
                store(NB - 2 + b, b)
            for b in range(2):
                sp.wait_ge(h2_kept[b], 16 * (NB // 2))

        @block.gpsimd
        def _(pool):
            def first(n, b, i):
                pool.wait_ge(x_in[b], 16 * i + 16)
                need(pool, x1_v, n - 1)
                pool.wait_ge(bog_v, 1)
                nc.gpsimd.tensor_tensor(xb[b][:, :, :], x[b][:, :, :],
                                        bog[:, bass.ds(n, 1), :].to_broadcast([P, C, E]), ALU.add).then_inc(xb_p, 1)

            def second(n, b, i):
                pool.wait_ge(xn_v, n + 1)
                need(pool, h2_rows_p, n)
                pool.wait_ge(bog_v, 1)
                nc.gpsimd.tensor_tensor(scaled[:, :, :], xn[b][:, :, :],
                                        rows[:, 2, bass.ds(n, 1), :].to_broadcast([P, C, E]), ALU.mult).then_inc(scaled_p, 1)
                pool.wait_ge(scaled_p, n + 1)
                pool.wait_ge(bog_v, 1)
                nc.gpsimd.tensor_tensor(h2_rows[:, bass.ds(n * C, C), 0:E], scaled[:, :, :],
                                        rows[:, 1, bass.ds(n, 1), :].to_broadcast([P, C, E]), ALU.add).then_inc(h2_rows_p, 1)

            steps(pool, first, second)

        @block.vector
        def _(dve):
            nc.vector.tensor_copy(silus[:, :, :], silu[:, :].unsqueeze(2).to_broadcast([P, NB, P])).then_inc(wide_v, 1)
            dve.wait_ge(rows_mm, 1)
            raw = lambda j: ps[:, :, j * E:j * E + E]
            nc.vector.tensor_copy(rows[:, 1, :, :], raw(1))
            nc.vector.tensor_scalar(rows[:, 2, :, :], raw(2), 1.0, None, ALU.add)
            for k, j in enumerate((0, 3)):
                if k:
                    dve.wait_ge(rows_v, 4)
                nc.vector.tensor_scalar(sign[:, :, :], raw(j), 0.0, 2.0, ALU.is_ge, ALU.mult)
                nc.vector.tensor_scalar(size[:, :, :], raw(j), -1.0, None, ALU.mult).then_inc(rows_v, 1)
                dve.wait_ge(rows_v, 4 * k + 1)
                nc.vector.tensor_tensor(size[:, :, :], size[:, :, :], raw(j), ALU.max).then_inc(rows_v, 1)
                dve.wait_ge(rows_v, 4 * k + 2)
                nc.vector.tensor_scalar(size[:, :, :], size[:, :, :], 0.25, None, ALU.max).then_inc(rows_v, 1)
                dve.wait_ge(rows_v, 4 * k + 3)
                nc.vector.scalar_tensor_tensor(rows[:, j, :, :], sign[:, :, :], -1.0, size[:, :, :],
                                               ALU.add, ALU.mult).then_inc(rows_v, 1)
            dve.wait_ge(rows_v, 8)
            dve.wait_ge(w_in, 64)
            nc.vector.tensor_tensor(bog[:, :, :], rows[:, 0, :, :],
                                    bo[:, :].unsqueeze(1).to_broadcast([P, NB, E]), ALU.mult).then_inc(bog_v, 1)
            nc.vector.tensor_tensor(wog[:, :, :], rows[:, 0, :, :],
                                    wo[:, :].unsqueeze(1).to_broadcast([P, NB, E]), ALU.mult).then_inc(wog_v, 1)

            def first(n, b, i):
                dve.wait_ge(xb_p, n + 1)
                dve.wait_ge(proj_mm, n + 1)
                nc.vector.tensor_tensor(x1[:, bass.ds(n, 1), :, :].rearrange("p o c e -> p (o c e)"), pB,
                                        flat(xb[b][:, :, :]), ALU.add).then_inc(x1_v, 1)
                dve.wait_ge(x1_v, n + 1)
                need(dve, h2_a, n - 1)
                nc.vector.tensor_scalar(now[b][:, :, :], mod[:, 3:5, bass.ds(n, 1)], 1.0, None, ALU.mult)
                base = n * (C + 3)
                for c in range(C):
                    nc.vector.bn_stats(stats[:, c, :],
                                       x1[:, bass.ds(n, 1), c, :].rearrange("p o e -> p (o e)")).then_inc(ln_v, 1)
                moments(nc, dve, stats, mean[:, :], tmp, var[:, :], ln_v, base + C, var_v)
                dve.wait_ge(std_a, n + 1)
                nc.vector.reciprocal(rstd[:, :], std[:, :]).then_inc(ln_v, 1)
                need(dve, h2_rows_p, n - 1)
                need(dve, xn_tr, n - 1)
                dve.wait_ge(ln_v, base + C + 3)
                for c in range(C):
                    last = nc.vector.tensor_scalar(xn[b][:, c, :],
                                                   x1[:, bass.ds(n, 1), c, :].rearrange("p o e -> p (o e)"),
                                                   mean[:, c:c + 1], rstd[:, c:c + 1], ALU.subtract, ALU.mult)
                last.then_inc(xn_v, 1)

            def second(n, b, i):
                dve.wait_ge(logit_mm, n + 1)
                dve.wait_ge(bog_v, 1)
                nc.vector.tensor_copy(logits[:, bass.ds(n, 1), :, :].rearrange("p o c e -> p (o c e)"),
                                      pD).then_inc(logit_v, 1)

            steps(dve, first, second)

        @block.scalar
        def _(act):
            def ahead(n, b, i):
                act.wait_ge(o_tr, n + 1)
                need(act, proj_mm, n)
                nc.scalar.activation(attn[:, :], pA, ACT.Identity).then_inc(attn_a, 1)

            def second(n, b, i):
                act.wait_ge(xn_tr, n + 1)
                need(act, logit_mm, n - 1)
                need(act, h2_kept[b], 16 * i)
                nc.scalar.activation(h2[b][:, :], pC, ACT.Identity, bias=now[b][:, 0, :],
                                     scale=now[b][:, 1, :]).then_inc(h2_a, 1)

            def deviation(n):
                act.wait_ge(var_v, n + 1)
                nc.scalar.activation(std[:, :], var[:, :], ACT.Sqrt).then_inc(std_a, 1)

            steps_ahead(act, None, ahead, second, deviation)

        @block.tensor
        def _(pe):
            pe.wait_ge(w_in, 64)
            pe.wait_ge(wide_v, 1)
            for n in range(NB):
                last = nc.tensor.matmul(ps[:, n, :], silus[:, n, :], wmod[:, :], start=True, stop=True)
            last.then_inc(rows_mm, 1)
            pe.wait_ge(rows_v, 8)

            def ahead(n, b, i):
                pe.wait_ge(o_in[b], 16 * i + 16)
                need(pe, attn_a, n)
                for c in range(C):
                    last = nc.tensor.transpose(pA[:, c * P:c * P + P], o[b][:, c, :], ident[:, :])
                last.then_inc(o_tr, 1)

            def first(n, b):
                if isinstance(n, int) and n == 0:
                    pe.wait_ge(wog_v, 1)
                need(pe, x1_v, n)
                pe.wait_ge(attn_a, n + 1)
                for c in range(C):
                    last = nc.tensor.matmul(pB[:, c * P:c * P + P], attn[:, c * P:c * P + P], wog[:, bass.ds(n, 1), :].rearrange("p o e -> p (o e)"),
                                            start=True, stop=True)
                last.then_inc(proj_mm, 1)

            def second(n, b, i):
                need(pe, h2_a, n)
                pe.wait_ge(xn_v, n + 1)
                for c in range(C):
                    last = nc.tensor.transpose(pC[:, c * P:c * P + P], xn[b][:, c, :], ident[:, :])
                last.then_inc(xn_tr, 1)
                need(pe, logit_v, n)
                pe.wait_ge(h2_a, n + 1)
                for c in range(C):
                    last = nc.tensor.matmul(pD[:, c * NX:c * NX + NX], h2[b][:, c * P:c * P + P], gw[:, :],
                                            start=True, stop=True)
                last.then_inc(logit_mm, 1)

            steps_ahead(pe, first, ahead, second)


def route(nc, io, keep, ps):
    T = NB * C
    logits, weight, slot, block_expert, h2_rows, ids = (
        keep[k] for k in ("logits", "weight", "slot", "block_expert", "h2_rows", "ids"))
    with ExitStack() as ctx:
        sb = lambda n, s, d=F32: ctx.enter_context(nc.sbuf_tensor("route_" + n, s, d))
        sem = lambda n: ctx.enter_context(nc.semaphore("route_" + n))
        gb, rank = sb("gate_b_rows", [P, NX]), sb("rank_rows", [P, NX])
        steps_of, block_no = sb("block_starts", [P, S * NB // BT]), sb("block_numbers", [P, BLOCKS])
        upper, ones = sb("upper", [P, P]), sb("ones", [P, P])
        lg = sb("lg", [P, T, NX])
        pick = [sb(f"pick{k}", [P, T, NX]) for k in range(2)]
        work = sb("work", [P, T, NX])
        top = [sb(f"top{k}", [P, T]) for k in range(2)]
        first, gap = sb("first", [P, T]), sb("gap", [P, T])
        taken = sb("taken", [P, NX, T])
        scan = [sb(f"scan{k}", [P, NX, T]) for k in range(2)]
        total = sb("total", [P, NX])
        count, over = sb("count", [P, NX]), sb("over", [P, NX, S * NB // BT])
        ends = [sb(f"ends{k}", [P, NX]) for k in range(4)]
        base, past, slot_f = sb("base", [P, NX]), sb("past", [P, BLOCKS, NX]), sb("slot_f", [P, T])
        expert_f = sb("expert_f", [P, BLOCKS])
        in_, v, gap_v, exp_a, total_v, count_mm = (
            sem("const_in"), sem("v"), sem("gap_v"), sem("gap_exp"), sem("total_v"), sem("count_mm"))
        before, counts = ps[:, 0, 0:NX], ps[:, 1, 0:NX]
        block = ctx.enter_context(nc.Block())

        @block.sync
        def _(sp):
            for dst, name in ((gb, "gate_b"), (rank, "rank"), (steps_of, "block_starts"), (block_no, "block_numbers")):
                sp.dma_start(dst[:, :], io[name].partition_broadcast(P)).then_inc(in_, 16)
            for dst, name in ((upper, "upper"), (ids, "token_ids")):
                sp.dma_start(dst[:, :], io[name]).then_inc(in_, 16)

        @block.scalar
        def _(act):
            act.wait_ge(gap_v, 1)
            nc.scalar.activation(gap[:, :], gap[:, :], ACT.Exp).then_inc(exp_a, 1)

        @block.vector
        def _(dve):
            done = [0]

            def step(instruction):
                done[0] += 1
                instruction.then_inc(v, 1)
                dve.wait_ge(v, done[0])

            tt, ts = nc.vector.tensor_tensor, nc.vector.tensor_scalar
            over_t = lambda ap: ap.unsqueeze(1).to_broadcast([P, T, NX])
            over_e = lambda ap: ap.unsqueeze(2).to_broadcast([P, T, NX])
            nc.vector.memset(ones[:, :], 1.0)
            dve.wait_ge(in_, 96)
            step(tt(lg[:, :, :], logits[:, :, :, :].rearrange("p n c e -> p (n c) e"), over_t(gb[:, :]), ALU.add))
            for k in range(2):
                step(nc.vector.tensor_reduce(top[k][:, :], lg[:, :, :], AX.X, ALU.max))
                step(tt(work[:, :, :], lg[:, :, :], over_e(top[k][:, :]), ALU.is_ge))
                step(tt(work[:, :, :], work[:, :, :], over_t(rank[:, :]), ALU.mult))
                step(nc.vector.tensor_reduce(first[:, :], work[:, :, :], AX.X, ALU.max))
                step(tt(pick[k][:, :, :], work[:, :, :], over_e(first[:, :]), ALU.is_equal))
                if k == 0:
                    step(nc.vector.scalar_tensor_tensor(lg[:, :, :], pick[0][:, :, :], -3.0e38, lg[:, :, :],
                                                        ALU.mult, ALU.add))
            tt(gap[:, :], top[1][:, :], top[0][:, :], ALU.subtract).then_inc(gap_v, 1)
            by_expert = lambda ap: ap.rearrange("p t e -> p e t")
            step(tt(taken[:, :, :], by_expert(pick[0][:, :, :]), by_expert(pick[1][:, :, :]), ALU.add))
            now = taken
            for k in range(6):
                d, new = 2 ** k, scan[k % 2]
                nc.vector.tensor_copy(new[:, :, 0:d], now[:, :, 0:d])
                step(tt(new[:, :, d:T], now[:, :, d:T], now[:, :, 0:T - d], ALU.add))
                now = new
            nc.vector.tensor_copy(total[:, :], now[:, :, T - 1]).then_inc(total_v, 1)
            step(tt(scan[0][:, :, :], now[:, :, :], taken[:, :, :], ALU.subtract))
            now = scan[0]
            dve.wait_ge(exp_a, 1)
            step(ts(weight[:, 0, :], gap[:, :], 1.0, None, ALU.add))
            step(nc.vector.reciprocal(weight[:, 0, :], weight[:, 0, :]))
            step(tt(weight[:, 1, :], weight[:, 0, :], gap[:, :], ALU.mult))
            dve.wait_ge(count_mm, 1)
            step(nc.vector.tensor_copy(count[:, :], counts))
            m = S * NB // BT
            step(tt(over[:, :, :], count[:, :].unsqueeze(2).to_broadcast([P, NX, m]),
                    steps_of[:, :].unsqueeze(1).to_broadcast([P, NX, m]), ALU.is_gt))
            step(nc.vector.tensor_reduce(ends[0][:, :], over[:, :, :], AX.X, ALU.add))
            for k in range(3):
                d = 2 ** k
                nc.vector.tensor_copy(ends[k + 1][:, 0:d], ends[k][:, 0:d])
                step(tt(ends[k + 1][:, d:NX], ends[k][:, d:NX], ends[k][:, 0:NX - d], ALU.add))
            step(tt(base[:, :], ends[3][:, :], ends[0][:, :], ALU.subtract))
            step(ts(base[:, :], base[:, :], float(BT), None, ALU.mult))
            step(tt(base[:, :], base[:, :], before, ALU.add))
            step(tt(now[:, :, :], now[:, :, :], base[:, :].unsqueeze(2).to_broadcast([P, NX, T]), ALU.add))
            for k in range(2):
                step(tt(work[:, :, :], pick[k][:, :, :], now[:, :, :].rearrange("p e t -> p t e"), ALU.mult))
                step(nc.vector.tensor_reduce(slot_f[:, :], work[:, :, :], AX.X, ALU.add))
                step(nc.vector.tensor_copy(slot[:, k, :], slot_f[:, :]))
            step(tt(past[:, :, :], block_no[:, :].unsqueeze(2).to_broadcast([P, BLOCKS, NX]),
                    ends[3][:, :].unsqueeze(1).to_broadcast([P, BLOCKS, NX]), ALU.is_ge))
            step(nc.vector.tensor_reduce(expert_f[:, :], past[:, :, :], AX.X, ALU.add))
            step(ts(expert_f[:, :], expert_f[:, :], float(NX - 1), None, ALU.min))
            step(nc.vector.tensor_copy(block_expert[:, :], expert_f[:, :]))
            nc.vector.tensor_copy(h2_rows[:, :, E], ids[:, :])
            step(nc.vector.tensor_copy(h2_rows[:, :, E + 1], weight[:, 0, :]))

        @block.tensor
        def _(pe):
            pe.wait_ge(in_, 96)
            pe.wait_ge(total_v, 1)
            nc.tensor.matmul(before, upper[:, :], total[:, :], start=True, stop=True)
            nc.tensor.matmul(counts, ones[:, :], total[:, :], start=True, stop=True).then_inc(count_mm, 1)


def dispatch(nc, io, scr, keep, ps):
    x1, h2T, h2_rows, rows, weight, slot, ids = (
        keep[k] for k in ("x1", "h2T", "h2_rows", "rows", "weight", "slot", "ids"))
    T, Q = NB * C, BT // P
    with ExitStack() as ctx:
        sb = lambda n, s, d=F32: ctx.enter_context(nc.sbuf_tensor("shared_" + n, s, d))
        sem = lambda n: ctx.enter_context(nc.semaphore("shared_" + n))
        w1, w2, b1, b2 = sb("w1", [P, HID]), sb("w2", [P, HC, E]), sb("b1", [P, HC]), sb("b2_rows", [P, E])
        hid = [sb(f"hid{b}", [P, HC, BT]) for b in range(2)]
        part = [sb(f"part{b}", [P, Q, E]) for b in range(2)]
        w_in, up_mm, gelu_a, down_mm, biased_v, gated_v, x1_v = (
            sem("w_in"), sem("up_mm"), sem("gelu_a"), sem("down_mm"), sem("biased_v"), sem("gated_v"), sem("x1_v"))
        sent = [sem(f"rows_sent{k}") for k in range(2)]
        second_v = sem("second_choice_v")
        up = [ps[:, j, :] for j in range(HC)]
        down = [ps[:, 4 + b, :] for b in range(2)]
        block = ctx.enter_context(nc.Block())

        @block.sync
        def _(sp):
            sp.dma_start(w1[:, :], io["ws1"]).then_inc(w_in, 16)
            sp.dma_start(w2[:, :, :], io["ws2"].rearrange("(c p) d -> p c d", p=P)).then_inc(w_in, 16)
            sp.dma_start(b1[:, :], io["bs1T"]).then_inc(w_in, 16)
            sp.dma_start(b2[:, :], io["bs2"].partition_broadcast(P)).then_inc(w_in, 16)

        @block.gpsimd
        def _(pool):
            for k in range(2):
                if k:
                    pool.wait_ge(second_v, 2)
                for t in range(T):
                    nc.gpsimd.indirect_dma_start(
                        scr["slots"], bass.IndirectOffsetOnAxis(ap=slot[:, k, t:t + 1], axis=0),
                        h2_rows[:, t, :], None).then_inc(sent[k], 16)
            pool.wait_ge(sent[1], 16 * T)

        @block.tensor
        def _(pe):
            def ups(n, b):
                k = 2 * n + b
                for j in range(HC):
                    need(pe, gelu_a, (k - 1) * HC + j + 1)
                    nc.tensor.matmul(up[j], w1[:, j * P:j * P + P],
                                     h2T[:, bass.ds(n, 1), b * BT:b * BT + BT].rearrange("p o s -> p (o s)"),
                                     start=True, stop=True).then_inc(up_mm, 1)

            def downs(n, b):
                k = 2 * n + b
                need(pe, biased_v, k - 1)
                pe.wait_ge(gelu_a, k * HC + HC)
                for q in range(Q):
                    for j in range(HC):
                        last = nc.tensor.matmul(down[b][:, q * E:q * E + E], hid[b][:, j, q * P:q * P + P],
                                                w2[:, j, :], start=j == 0, stop=j == HC - 1)
                last.then_inc(down_mm, 1)

            pe.wait_ge(w_in, 64)
            ups(0, 0)
            ups(0, 1)
            downs(0, 0)
            with pe.Fori(1, NB) as n:
                ups(n, 0)
                downs(n - 1, 1)
                ups(n, 1)
                downs(n, 0)
            downs(NB - 1, 1)

        @block.scalar
        def _(act):
            act.wait_ge(w_in, 64)

            def gelus(n, b):
                k = 2 * n + b
                need(act, down_mm, k - 1)
                for j in range(HC):
                    act.wait_ge(up_mm, k * HC + j + 1)
                    nc.scalar.activation(hid[b][:, j, :], up[j], ACT.Gelu, bias=b1[:, j:j + 1]).then_inc(gelu_a, 1)

            for b in range(2):
                gelus(0, b)
            with act.Fori(1, NB) as n:
                for b in range(2):
                    gelus(n, b)

        @block.vector
        def _(dve):
            def add(n, b):
                k = 2 * n + b
                here = x1[:, bass.ds(n, 1), b * Q:b * Q + Q, :].rearrange("p o c e -> p (o c) e")
                need(dve, x1_v, k - 1)
                dve.wait_ge(down_mm, k + 1)
                nc.vector.tensor_tensor(part[b][:, :, :], down[b].rearrange("p (q e) -> p q e", q=Q),
                                        b2[:, :].unsqueeze(1).to_broadcast([P, Q, E]), ALU.add).then_inc(biased_v, 1)
                dve.wait_ge(biased_v, k + 1)
                nc.vector.tensor_tensor(part[b][:, :, :], part[b][:, :, :],
                                        rows[:, 3, bass.ds(n, 1), :].to_broadcast([P, Q, E]), ALU.mult).then_inc(gated_v, 1)
                dve.wait_ge(gated_v, k + 1)
                nc.vector.tensor_tensor(here, here, part[b][:, :, :], ALU.add).then_inc(x1_v, 1)

            dve.wait_ge(w_in, 64)
            for b in range(2):
                add(0, b)
            with dve.Fori(1, NB // 2) as n:
                for b in range(2):
                    add(n, b)
            dve.wait_ge(sent[0], 16 * T)
            nc.vector.tensor_scalar(h2_rows[:, :, E], ids[:, :], float(NB * S), None, ALU.add).then_inc(second_v, 1)
            nc.vector.tensor_copy(h2_rows[:, :, E + 1], weight[:, 1, :]).then_inc(second_v, 1)
            with dve.Fori(NB // 2, NB) as n:
                for b in range(2):
                    add(n, b)


def experts(nc, io, scr, keep, ident, ps):
    block_expert = keep["block_expert"]
    Q, RING, TURNS = BT // P, 3, BLOCKS // 3
    with ExitStack() as ctx:
        sb = lambda n, s, d=F32: ctx.enter_context(nc.sbuf_tensor("expert_" + n, s, d))
        sem = lambda n: ctx.enter_context(nc.semaphore("expert_" + n))
        w = [sb(f"w{b}", [P, 2 * HID + HC]) for b in range(RING)]
        b2 = [sb(f"b2_rows{b}", [P, E]) for b in range(RING)]
        x = [sb(f"x{b}", [P, Q, E + 2]) for b in range(RING)]
        xT = [sb(f"xT{b}", [P, BT]) for b in range(RING)]
        hid = [sb(f"hid{b}", [P, HC, BT]) for b in range(RING)]
        biased = [sb(f"biased{b}", [P, Q, E]) for b in range(RING)]
        y = [sb(f"y{b}", [P, Q, E]) for b in range(RING)]
        spare = sb("spare_rows", [P, BLOCKS * Q])
        empty = [sb(f"empty{b}", [P, Q]) for b in range(RING)]
        row = [sb(f"row{b}", [P, Q], I32) for b in range(RING)]
        weight = [sb(f"weight{b}", [P, Q]) for b in range(RING)]
        w_in = [sem(f"w_in{b}") for b in range(RING)]
        x_in = [sem(f"x_in{b}") for b in range(RING)]
        spare_in, x_tr, xT_v, up_mm, gelu_a, down_mm, empty_v, row_v, biased_v, y_v = (
            sem("spare_in"), sem("x_tr"), sem("xT_v"), sem("up_mm"), sem("gelu_a"), sem("down_mm"),
            sem("empty_v"), sem("row_v"), sem("biased_v"), sem("y_v"))
        y_sent, y_seen = [sem(f"y_sent{b}") for b in range(RING)], sem("y_seen")
        up = [ps[:, j, :] for j in range(HC)]
        down = [ps[:, 4 + b, :] for b in range(RING)]
        tr = ps[:, 7, :]
        slots = scr["slots"].rearrange("(m p q) e -> m p q e", p=P, q=Q)
        block = ctx.enter_context(nc.Block())

        @block.sync
        def _(sp):
            sp.dma_start(spare[:, :], io["spare_rows"]).then_inc(spare_in, 16)

            def load_x(m, b):
                sp.dma_start(x[b][:, :, :], slots[m]).then_inc(x_in[b], 16)

            def load_w(m, b):
                e = sp.value_load(block_expert[0:1, bass.ds(m, 1)], min_val=0, max_val=NX - 1)
                sp.dma_start(w[b][:, :], io["w_pack"][bass.ds(e, 1)].rearrange("o p k -> p (o k)")).then_inc(w_in[b], 16)
                sp.dma_start(b2[b][:, :], io["b2"][bass.ds(e, 1)].rearrange("o k -> (o k)").partition_broadcast(P)).then_inc(w_in[b], 16)

            for b in range(RING):
                load_x(b, b)
                load_w(b, b)
            with sp.Fori(1, TURNS) as i:
                for b in range(RING):
                    m = RING * i + b
                    sp.wait_ge(row_v, m - RING + 1)
                    load_x(m, b)
                    sp.wait_ge(biased_v, m - RING + 1)
                    load_w(m, b)

        def steps(engine, one):
            for b in range(RING):
                one(b, b, 0)
            with engine.Fori(1, TURNS) as i:
                for b in range(RING):
                    one(RING * i + b, b, i)

        @block.gpsimd
        def _(pool):
            def one(m, b, i):
                pool.wait_ge(y_v, m + 1)
                pool.sem_inc(y_seen, 1)
                for q in range(Q):
                    nc.gpsimd.indirect_dma_start(
                        scr["results"], bass.IndirectOffsetOnAxis(ap=row[b][:, q:q + 1], axis=0),
                        y[b][:, q, :], None).then_inc(y_sent[b], 16)

            steps(pool, one)
            for b in range(RING):
                pool.wait_ge(y_sent[b], 16 * Q * TURNS)

        @block.tensor
        def _(pe):
            def turn(m, b, i):
                need(pe, xT_v, m)
                pe.wait_ge(x_in[b], 16 * i + 16)
                for q in range(Q):
                    last = nc.tensor.transpose(tr[:, q * P:q * P + P], x[b][:, q, 0:E], ident[:, :])
                last.then_inc(x_tr, 1)

            def ups(m, b, i):
                pe.wait_ge(w_in[b], 32 * i + 32)
                pe.wait_ge(xT_v, m + 1)
                for j in range(HC):
                    need(pe, gelu_a, (m - 1) * HC + j + 1)
                    nc.tensor.matmul(up[j], w[b][:, j * P:j * P + P], xT[b][:, :],
                                     start=True, stop=True).then_inc(up_mm, 1)

            def downs(m, b):
                need(pe, biased_v, m - RING + 1)
                pe.wait_ge(gelu_a, m * HC + HC)
                for q in range(Q):
                    for j in range(HC):
                        last = nc.tensor.matmul(down[b][:, q * E:q * E + E], hid[b][:, j, q * P:q * P + P],
                                                w[b][:, HID + j * E:HID + j * E + E], start=j == 0, stop=j == HC - 1)
                last.then_inc(down_mm, 1)

            def one(m, b, i):
                ups(m, b, i)
                if b < RING - 1:
                    turn(m + 1, b + 1, i)
                elif not isinstance(m, int) or m + 1 < BLOCKS:
                    turn(m + 1, 0, i + 1)
                if not isinstance(m, int) or m > 0:
                    downs(m - 1, (b - 1) % RING)

            turn(0, 0, 0)
            for b in range(RING):
                one(b, b, 0)
            with pe.Fori(1, TURNS - 1) as i:
                for b in range(RING):
                    one(RING * i + b, b, i)
            for b in range(RING):
                one(BLOCKS - RING + b, b, TURNS - 1)
            downs(BLOCKS - 1, RING - 1)

        @block.scalar
        def _(act):
            def one(m, b, i):
                need(act, down_mm, m - RING + 1)
                for j in range(HC):
                    act.wait_ge(up_mm, m * HC + j + 1)
                    nc.scalar.activation(hid[b][:, j, :], up[j], ACT.Gelu,
                                         bias=w[b][:, 2 * HID + j:2 * HID + j + 1]).then_inc(gelu_a, 1)

            steps(act, one)

        @block.vector
        def _(dve):
            def prepare(m, b, i):
                need(dve, down_mm, m - RING + 1)
                dve.wait_ge(x_tr, m + 1)
                nc.vector.tensor_copy(xT[b][:, :], tr).then_inc(xT_v, 1)
                ids = x[b][:, :, E]
                dve.wait_ge(spare_in, 16)
                nc.vector.scalar_tensor_tensor(empty[b][:, :], ids, 0.0, spare[:, bass.ds(m * Q, Q)],
                                               ALU.is_equal, ALU.mult).then_inc(empty_v, 1)
                need(dve, y_v, m - RING + 1)
                nc.vector.tensor_copy(weight[b][:, :], x[b][:, :, E + 1])
                need(dve, y_sent[b], 16 * Q * i)
                dve.wait_ge(empty_v, m + 1)
                nc.vector.scalar_tensor_tensor(row[b][:, :], ids, -1.0, empty[b][:, :],
                                               ALU.add, ALU.add).then_inc(row_v, 1)

            def finish(m, b):
                need(dve, y_v, m - RING + 1)
                dve.wait_ge(down_mm, m + 1)
                nc.vector.tensor_tensor(biased[b][:, :, :], down[b].rearrange("p (q e) -> p q e", q=Q),
                                        b2[b][:, :].unsqueeze(1).to_broadcast([P, Q, E]), ALU.add).then_inc(biased_v, 1)
                dve.wait_ge(row_v, m + 1)
                dve.wait_ge(biased_v, m + 1)
                for q in range(Q):
                    last = nc.vector.tensor_scalar(y[b][:, q, :], biased[b][:, q, :], weight[b][:, q:q + 1], None,
                                                   ALU.mult)
                last.then_inc(y_v, 1)

            def one(m, b, i):
                if b < RING - 1:
                    prepare(m + 1, b + 1, i)
                elif not isinstance(m, int) or m + 1 < BLOCKS:
                    prepare(m + 1, 0, i + 1)
                if not isinstance(m, int) or m > 0:
                    finish(m - 1, (b - 1) % RING)

            prepare(0, 0, 0)
            for b in range(RING):
                one(b, b, 0)
            with dve.Fori(1, TURNS - 1) as i:
                for b in range(RING):
                    one(RING * i + b, b, i)
            for b in range(RING):
                one(BLOCKS - RING + b, b, TURNS - 1)
            finish(BLOCKS - 1, RING - 1)


def combine(nc, io, scr, keep):
    x1, rows = keep["x1"], keep["rows"]
    with ExitStack() as ctx:
        sb = lambda n, s, d=F32: ctx.enter_context(nc.sbuf_tensor("combine_" + n, s, d))
        sem = lambda n: ctx.enter_context(nc.semaphore("combine_" + n))
        y = [[sb(f"y{k}_{b}", [P, C, E]) for k in range(2)] for b in range(2)]
        out = [sb(f"out{b}", [P, C, E]) for b in range(2)]
        y_in = [sem(f"y_in{b}") for b in range(2)]
        stored = [sem(f"stored{b}") for b in range(2)]
        sum_p, gated_v, out_v = sem("sum_p"), sem("gated_v"), sem("out_v")
        results = scr["results"][0:2 * NB * S].rearrange("(k n p c) e -> k n p c e", k=2, n=NB, p=P)
        out_dram = io["out"].rearrange("n (p c) e -> n p c e", c=C)
        block = ctx.enter_context(nc.Block())

        @block.sync
        def _(sp):
            def load(n, b):
                for k in range(2):
                    sp.dma_start(y[b][k][:, :, :], results[k, n]).then_inc(y_in[b], 16)

            for b in range(2):
                load(b, b)
            for n in range(NB):
                b = n % 2
                sp.wait_ge(out_v, n + 1)
                if n + 2 < NB:
                    load(n + 2, b)
                sp.dma_start(out_dram[n], out[b][:, :, :]).then_inc(stored[b], 16)
            for b in range(2):
                sp.wait_ge(stored[b], 16 * (NB // 2))

        @block.gpsimd
        def _(pool):
            for n in range(NB):
                b = n % 2
                pool.wait_ge(y_in[b], 32 * (n // 2) + 32)
                need(pool, stored[b], 16 * (n // 2))
                nc.gpsimd.tensor_tensor(out[b][:, :, :], y[b][0][:, :, :], y[b][1][:, :, :], ALU.add).then_inc(sum_p, 1)

        @block.vector
        def _(dve):
            for n in range(NB):
                b = n % 2
                dve.wait_ge(sum_p, n + 1)
                nc.vector.tensor_tensor(out[b][:, :, :], out[b][:, :, :],
                                        rows[:, 3, n:n + 1, :].to_broadcast([P, C, E]), ALU.mult).then_inc(gated_v, 1)
                dve.wait_ge(gated_v, n + 1)
                nc.vector.tensor_tensor(out[b][:, :, :], out[b][:, :, :], x1[:, n, :, :], ALU.add).then_inc(out_v, 1)


def block_kernel(nc, io, out):
    io = dict(io, out=out)
    T = NB * C
    with ExitStack() as ctx:
        sb = lambda n, s, d=F32: ctx.enter_context(nc.sbuf_tensor(n, s, d))
        ps = ctx.enter_context(nc.psum_tensor("ps", [P, 8, 512], F32))
        mod, ident, silu = sb("mod", [P, 6, NB]), sb("ident", [P, P]), sb("silu", [P, NB])
        ident_in = ctx.enter_context(nc.semaphore("ident_in"))
        scr = {
            "o": nc.dram_tensor("o_scratch", [NB, H, S * D], F32).ap(),
            "slots": nc.dram_tensor("slots_scratch", [BLOCKS * BT, E + 2], F32).ap(),
            "results": nc.dram_tensor("results_scratch", [2 * NB * S + BLOCKS * BT, E], F32).ap(),
        }
        with nc.Block() as block:
            @block.sync
            def _(sp):
                sp.dma_start(ident[:, :], io["ident"]).then_inc(ident_in, 16)
                sp.wait_ge(ident_in, 16)
        attend(nc, io, scr, mod, ident, silu, ps)
        keep = {
            "silu": silu, "x1": sb("x1", [P, NB, C, E]), "h2T": sb("h2T", [P, NB, S]),
            "h2_rows": sb("h2_rows", [P, T, E + 2]), "rows": sb("mod_rows", [P, 4, NB, E]),
            "logits": sb("logits", [P, NB, C, NX]), "weight": sb("weight", [P, 2, T]),
            "slot": sb("slot", [P, 2, T], I32), "ids": sb("ids", [P, T]),
            "block_expert": sb("block_expert", [P, BLOCKS], I32),
        }
        merge(nc, io, scr, keep, mod, ident, ps)
        route(nc, io, keep, ps)
        dispatch(nc, io, scr, keep, ps)
        experts(nc, io, scr, keep, ident, ps)
        combine(nc, io, scr, keep)


def kernel(**inputs):
    import numpy as np
    import concourse.bacc as bacc
    from concourse.bass_utils import run_bass_kernel_spmd

    a = {k[3:]: np.asarray(v) for k, v in inputs.items()}
    order = np.arange(E).reshape(H, D).T.reshape(-1)
    by_part = lambda w: w.reshape(NX, HC, P, E).transpose(0, 2, 1, 3).reshape(NX, P, HC * E)
    p, f32 = np.arange(P)[:, None], np.float32
    slot = (np.arange(BLOCKS)[:, None] * BT + np.arange(BT // P)).reshape(1, -1) + p * (BT // P)
    arrays = {
        "x": a["attn_x"], "cT": a["c"].T, "wmod": a["wmod"], "ident": np.eye(P, dtype=f32),
        "w_qkv": np.concatenate([a["attn_Wq"].T[:, order], a["attn_Wk"].T[:, order], a["attn_Wv"].T], 1),
        "b_qkv": np.concatenate([a["attn_bq"][order], a["attn_bk"][order], a["attn_bv"]]),
        "WoT": a["attn_Wo"].T, "bo": a["attn_bo"], "gate_w": a["ffn_gate_w"], "gate_b": a["ffn_gate_b"],
        "w_pack": np.concatenate([a["ffn_w1"], by_part(a["ffn_w2"]),
                                  a["ffn_b1"].reshape(NX, HC, P).transpose(0, 2, 1)], 2),
        "b2": a["ffn_b2"], "ws1": a["ffn_ws1"], "ws2": a["ffn_ws2"],
        "bs1T": a["ffn_bs1"].reshape(HC, P).T, "bs2": a["ffn_bs2"],
        "rank": np.arange(NX, 0, -1).astype(f32), "upper": np.triu(np.ones((P, P), f32), 1),
        "block_starts": (np.arange(NB * S // BT) * BT).astype(f32), "block_numbers": np.arange(BLOCKS).astype(f32),
        "token_ids": (1 + np.arange(NB)[None, :, None] * S + p[:, :, None] * C
                      + np.arange(C)).reshape(P, -1).astype(f32),
        "spare_rows": (1 + 2 * NB * S + slot).astype(f32),
    }
    arrays = {k: np.ascontiguousarray(v) for k, v in arrays.items()}
    nc = bacc.Bacc("TRN2", target_bir_lowering=False, num_devices=1)
    io = {k: nc.dram_tensor(f"in_{k}", v.shape, mybir.dt.from_np(v.dtype), kind="ExternalInput").ap()
          for k, v in arrays.items()}
    out = nc.dram_tensor("out", (NB, S, E), F32, kind="ExternalOutput").ap()
    block_kernel(nc, io, out)
    r = run_bass_kernel_spmd(nc, [{f"in_{k}": v for k, v in arrays.items()}], core_ids=[0])
    return r.results[0]["out"]
```

```python
from contextlib import ExitStack

import concourse.bass as bass
from concourse import mybir

F32, F32R, I32 = mybir.dt.float32, mybir.dt.float32r, mybir.dt.int32
ALU = mybir.AluOpType
ACT = mybir.ActivationFunctionType
AX = mybir.AxisListType

NB, S, E = 8, 1024, 128
P = 128
H, D = 16, 8
HH = H * H
C = S // P
CU = C // 2
SCALE = 1.0 / D ** 0.5
EPS = 1e-5
NX, HID = 8, 512
HC = HID // P
BT = 512
BLOCKS = 2 * NB * S // BT + NX - 1

RING = 3


def flat(ap):
    return ap.rearrange("p a b -> p (a b)")


def need(engine, semaphore, count):
    if not isinstance(count, int) or count > 0:
        engine.wait_ge(semaphore, count)


def moments(nc, dve, stats, mean, tmp, var, ln_v, base, ready):
    total, gap, squares = tmp
    dve.wait_ge(ln_v, base)
    nc.vector.tensor_tensor(total, stats[:, :, 1], stats[:, :, 4], ALU.add)
    nc.vector.tensor_tensor(gap, stats[:, :, 1], stats[:, :, 4], ALU.subtract)
    nc.vector.tensor_tensor(squares, stats[:, :, 2], stats[:, :, 5], ALU.add).then_inc(ln_v, 1)
    dve.wait_ge(ln_v, base + 1)
    nc.vector.tensor_scalar(mean, total, 0.5, None, ALU.mult)
    nc.vector.scalar_tensor_tensor(gap, gap, 0.25, gap, ALU.mult, ALU.mult)
    nc.vector.tensor_scalar(squares, squares, 1.0 / E, EPS, ALU.mult, ALU.add).then_inc(ln_v, 1)
    dve.wait_ge(ln_v, base + 2)
    nc.vector.tensor_tensor(var, gap, squares, ALU.add).then_inc(ready, 1)


def attend(nc, io, scr, mod, ident, rows, gated, ps):
    with ExitStack() as ctx:
        sb = lambda n, s, d=F32: ctx.enter_context(nc.sbuf_tensor("attend_" + n, s, d))
        sem = lambda n: ctx.enter_context(nc.semaphore("attend_" + n))
        cT, sig, silu = sb("cT", [P, NB]), sb("sig", [P, NB]), sb("silu", [P, NB])
        zeros, zeros_p, zeroed = sb("zeros", [P, BLOCKS, E + 2]), sem("zeros_p"), sem("slots_zeroed")
        wo, bo, wo_in = sb("woT", [P, E]), sb("bo_rows", [P, E]), sem("wo_in")
        modT = sb("modT", [4 * NB, E])
        wmod, raw = sb("wmod", [P, 6, E]), sb("raw_mod", [P, 6, NB])
        sgn, mag = sb("sgn", [P, 2, NB]), sb("mag", [P, 2, NB])
        wqkv, bqkv = sb("w_qkv", [P, 3 * E]), sb("b_qkv", [P, 3 * E])
        x = [sb(f"x{b}", [P, C, E]) for b in range(2)]
        stats, mean = sb("stats", [P, C, 6]), sb("mean", [P, C])
        tmp = [sb(f"moment_tmp{k}", [P, C])[:, :] for k in range(3)]
        var, std, rstd, offset = (sb(n, [P, C]) for n in ("var", "std", "rstd", "offset"))
        table, table_a = sb("table", [P, 1]), sem("table_a")
        shift = [sb(f"shift{b}", [P, 2, 1]) for b in range(2)]
        hT = sb("hT", [P, S])
        qkv = [sb(f"qkv{b}", [P, C, 3 * E]) for b in range(2)]
        QK_RING = CU
        qk_prod = [sb(f"qk_prod{r}", [P, D, H, H]) for r in range(QK_RING)]
        pv_pool = sb("pv_prod_pool", [P, H, H, D])
        DVE_PV = CU - 1
        pv_dve = [sb(f"pv_prod_dve{r}", [P, H, D, H]) for r in range(DVE_PV)]
        top, less = sb("row_max", [P, CU * H]), sb("less_max", [P, CU, HH])
        prob_sb = [sb(f"prob_last{g}", [P, HH]) for g in range(2)]
        total, recip = sb("row_sum", [P, CU * H]), sb("row_recip", [P, CU * H])
        sums = sb("sums", [P, DVE_PV, E])
        out = [sb(f"out{b}", [P, H, C, D]) for b in range(2)]

        small_in, wmod_in, exp_c, silu_v = sem("small_in"), sem("wmod_in"), sem("exp_neg_c"), sem("silu_v")
        mod_mm, mod_v, mod_tr, modT_v, mod_stored, rows_in = sem("mod_mm"), sem("mod_v"), sem("mod_tr"), sem("modT_v"), sem("mod_stored"), sem("rows_in")
        x_in = [sem(f"x_in{b}") for b in range(2)]
        ln_v, var_ready, std_ready, scale_v, v_ready = (
            sem("ln_v"), sem("var_ready"), sem("std_ready"), sem("scale_v"), sem("v_ready"))
        xn_ready, xt_mm, hT_done = sem("xn_ready"), sem("xt_mm"), sem("hT_done")
        qkv_mm, qkv_copied, qkv_ready = sem("qkv_mm"), sem("qkv_copied"), sem("qkv_ready")
        qk_prod_ready, qk_summed = sem("qk_prod_ready"), sem("qk_summed")
        top_v, less_v, prob_a, total_v, recip_v = (
            sem("row_max_v"), sem("less_max_v"), sem("prob_a"), sem("row_sum_v"), sem("row_recip_v"))
        pv_prod_ready, pv_summed = sem("pv_prod_ready"), sem("pv_summed")
        pv_mult_v, pv_sum_v, norm_v = sem("pv_mult_v"), sem("pv_sum_v"), sem("norm_v")
        stored = [sem(f"out_stored{b}") for b in range(2)]

        score = [ps[:, 2 * g:2 * g + 2, :].rearrange("p a (b s) -> p (a b) s", b=2) for g in range(2)]
        q_acc = [ps[:, 4 + j, 0:3 * E] for j in range(2)]
        t_acc, o_acc = ps[:, 6, :], ps[:, 7, 0:E]
        x_dram = io["x"].rearrange("n (p c) e -> n p c e", c=C)
        o_dram = scr["o"].rearrange("n h (p x) -> n p h x", p=P)
        block = ctx.enter_context(nc.Block())

        def steps(engine, batch):
            for b in range(2):
                batch(b, b)
            with engine.Fori(1, NB // 2 - 1) as i:
                for b in range(2):
                    batch(2 * i + b, b)
            for b in range(2):
                batch(NB - 2 + b, b, more=b == 0)

        @block.sync
        def _(sp):
            for dst, name in ((cT, "cT"), (wqkv, "w_qkv")):
                sp.dma_start(dst[:, :], io[name]).then_inc(small_in, 16)
            sp.dma_start(x[0][:, :, :], x_dram[0]).then_inc(x_in[0], 16)
            sp.dma_start(flat(wmod[:, :, :]), io["wmod"]).then_inc(wmod_in, 16)
            sp.dma_start(bqkv[:, :], io["b_qkv"].partition_broadcast(P)).then_inc(small_in, 16)
            sp.dma_start(x[1][:, :, :], x_dram[1]).then_inc(x_in[1], 16)
            sp.dma_start(bo[:, :], io["bo"].partition_broadcast(P)).then_inc(wo_in, 16)
            sp.dma_start(wo[:, :], io["WoT"]).then_inc(wo_in, 16)
            sp.wait_ge(modT_v, 1)
            sp.dma_start(scr["mod"].rearrange("j n e -> (j n) e"), modT[:, :]).then_inc(mod_stored, 16)
            sp.wait_ge(mod_stored, 16)
            sp.dma_start(rows[:, :, :, :].rearrange("p j n e -> p (j n e)"),
                         scr["mod"].rearrange("j n p -> (j n p)").partition_broadcast(P)).then_inc(rows_in, 16)
            sp.wait_ge(zeros_p, 1)
            slots = scr["slots"].rearrange("(q m p) e -> q p m e", q=BT // P, p=P)
            for q in range(BT // P):
                sp.dma_start(slots[q], zeros[:, :, :]).then_inc(zeroed, 16)

            def batch(t, b, more=True):
                if more:
                    sp.wait_ge(xt_mm, 2 * t + 2)
                    sp.dma_start(x[b][:, :, :], x_dram[t + 2]).then_inc(x_in[b], 16)
                sp.wait_ge(norm_v, 2 * t + 2)
                sp.dma_start(o_dram[t], out[b][:, :, :, :].rearrange("p h c d -> p h (c d)")).then_inc(stored[b], 16)

            with sp.Fori(0, NB // 2 - 1) as i:
                for b in range(2):
                    batch(2 * i + b, b)
            for b in range(2):
                batch(NB - 2 + b, b, more=False)
            for b in range(2):
                sp.wait_ge(stored[b], NB // 2 * 16)
            sp.wait_ge(zeroed, BT // P * 16)
            sp.wait_ge(rows_in, 16)

        @block.gpsimd
        def _(pool):
            def bias_qkv(t, b, cs):
                for c in cs:
                    pool.wait_ge(qkv_copied, t * C + c + 1)
                    nc.gpsimd.tensor_tensor(qkv[b][:, c, 0:2 * E], qkv[b][:, c, 0:2 * E], bqkv[:, 0:2 * E], ALU.add).then_inc(qkv_ready, 1)

            def score_products(t, b, g, js=range(CU)):
                for j in js:
                    c = g * CU + j
                    k = (2 * t + g) * CU + j
                    pool.wait_ge(qkv_ready, t * C + c + 1)
                    need(pool, qk_summed, k - QK_RING + 1)
                    q = qkv[b][:, c, 0:E].rearrange("p (d h) -> p d h", d=D)
                    kk = qkv[b][:, c, E:2 * E].rearrange("p (d h) -> p d h", d=D)
                    nc.gpsimd.tensor_tensor(
                        qk_prod[c % QK_RING][:, :, :, :],
                        q.unsqueeze(3).to_broadcast([P, D, H, H]), kk.unsqueeze(2).to_broadcast([P, D, H, H]),
                        ALU.mult).then_inc(qk_prod_ready, 1)

            def value_products(t, b, g):
                v = 2 * t + g
                c = g * CU + CU - 1
                pool.wait_ge(prob_a, 2 * v + 1)
                pool.wait_ge(v_ready, v + 1)
                need(pool, pv_summed, v)
                pr = prob_sb[g][:, :].rearrange("p (q k) -> p k q", q=H)
                val = qkv[b][:, c, 2 * E:3 * E].rearrange("p (k d) -> p k d", k=H)
                nc.gpsimd.tensor_tensor(
                    pv_pool[:, :, :, :],
                    pr.unsqueeze(3).to_broadcast([P, H, H, D]), val.unsqueeze(2).to_broadcast([P, H, H, D]),
                    ALU.mult).then_inc(pv_prod_ready, 1)

            def batch(t, b, more=True):
                score_products(t, b, 1)
                value_products(t, b, 0)
                if more:
                    bias_qkv(t + 1, 1 - b, range(1))
                    for j in range(CU - 1):
                        score_products(t + 1, 1 - b, 0, range(j, j + 1))
                        bias_qkv(t + 1, 1 - b, range(j + 1, j + 2))
                    bias_qkv(t + 1, 1 - b, range(CU, CU + 1))
                    score_products(t + 1, 1 - b, 0, range(CU - 1, CU))
                    bias_qkv(t + 1, 1 - b, range(CU + 1, CU + 2))
                value_products(t, b, 1)
                if more:
                    bias_qkv(t + 1, 1 - b, range(CU + 2, C))

            nc.gpsimd.memset(zeros[:, :, :], 0.0).then_inc(zeros_p, 1)
            bias_qkv(0, 0, range(1))
            for c in range(CU):
                score_products(0, 0, 0, range(c, c + 1))
                bias_qkv(0, 0, range(c + 1, c + 2))
            bias_qkv(0, 0, range(CU + 1, C))
            steps(pool, batch)
            pool.wait_ge(rows_in, 16)
            pool.wait_ge(wo_in, 32)
            for dst, source in zip(gated, (bo, wo)):
                nc.gpsimd.tensor_tensor(dst[:, :, :], rows[:, 0, :, :],
                                        source[:, :].unsqueeze(1).to_broadcast([P, NB, E]), ALU.mult)

        @block.scalar
        def _(act):
            act.wait_ge(small_in, 48)
            nc.scalar.activation(sig[:, :], cT[:, :], ACT.Exp, scale=-1.0).then_inc(exp_c, 1)

            def deviation(t):
                act.wait_ge(var_ready, t + 1)
                nc.scalar.activation(std[:, :], var[:, :], ACT.Sqrt).then_inc(std_ready, 1)

            def normalise(t, b):
                act.wait_ge(scale_v, t + 1)
                for c in range(C):
                    last = nc.scalar.activation(x[b][:, c, :], x[b][:, c, :], ACT.Identity,
                                                bias=offset[:, c:c + 1], scale=rstd[:, c:c + 1])
                last.then_inc(xn_ready, 1)

            def modulate(t, b):
                for r in range(2):
                    act.wait_ge(xt_mm, 2 * t + r + 1)
                    need(act, qkv_mm, t * C)
                    nc.scalar.activation(hT[:, r * 512:r * 512 + 512], t_acc, ACT.Identity,
                                         bias=shift[b][:, 0, :], scale=shift[b][:, 1, :]).then_inc(hT_done, 1)

            def copy_qkv(t, b, cs):
                for c in cs:
                    need(act, pv_mult_v, DVE_PV * (2 * t - 2))
                    need(act, pv_prod_ready, 2 * t - 2)
                    act.wait_ge(qkv_mm, t * C + c + 1)
                    nc.scalar.activation(qkv[b][:, c, :], q_acc[c % 2], ACT.Identity).then_inc(qkv_copied, 1)

            def probabilities(t, g):
                v = 2 * t + g
                act.wait_ge(less_v, v + 1)
                need(act, pv_prod_ready, v - 1)
                nc.scalar.activation(prob_sb[g][:, :], less[:, CU - 1, :], ACT.Exp, scale=SCALE).then_inc(prob_a, 1)
                nc.scalar.activation(score[g][:, 0:DVE_PV, :], less[:, 0:DVE_PV, :], ACT.Exp,
                                     scale=SCALE).then_inc(prob_a, 1)

            def batch(t, b, more=True, far=True):
                probabilities(t, 0)
                if more:
                    modulate(t + 1, 1 - b)
                    copy_qkv(t + 1, 1 - b, range(2))
                probabilities(t, 1)
                if more:
                    copy_qkv(t + 1, 1 - b, range(2, CU + 1))
                if far:
                    deviation(t + 2)
                    need(act, table_a, t)
                    nc.scalar.activation(table[:, :], cT[:, 0:1], ACT.Exp).then_inc(table_a, 1)
                if more:
                    copy_qkv(t + 1, 1 - b, range(CU + 1, CU + 2))
                if far:
                    normalise(t + 2, b)
                if more:
                    copy_qkv(t + 1, 1 - b, range(CU + 2, C))

            deviation(0)
            normalise(0, 0)
            modulate(0, 0)
            copy_qkv(0, 0, range(C))
            deviation(1)
            normalise(1, 1)
            for b in range(2):
                batch(b, b)
            with act.Fori(1, NB // 2 - 1) as i:
                for b in range(2):
                    batch(2 * i + b, b)
            for b in range(2):
                batch(NB - 2 + b, b, more=b == 0, far=False)

        @block.vector
        def _(dve):
            dve.wait_ge(exp_c, 1)
            nc.vector.tensor_scalar(sig[:, :], sig[:, :], 1.0, None, ALU.add).then_inc(silu_v, 1)
            dve.wait_ge(silu_v, 1)
            nc.vector.reciprocal(sig[:, :], sig[:, :]).then_inc(silu_v, 1)
            dve.wait_ge(silu_v, 2)
            nc.vector.tensor_tensor(silu[:, :], cT[:, :], sig[:, :], ALU.mult).then_inc(silu_v, 1)
            LN = C + 3

            def statistics(t, b, full):
                dve.wait_ge(x_in[b], full)
                for c in range(C):
                    nc.vector.bn_stats(stats[:, c, :], x[b][:, c, :]).then_inc(ln_v, 1)
                moments(nc, dve, stats, mean[:, :], tmp, var[:, :], ln_v, t * LN + C, var_ready)

            def scales(t, b):
                nc.vector.tensor_copy(shift[b][:, :, :], mod[:, 0:2, bass.ds(t, 1)])
                dve.wait_ge(std_ready, t + 1)
                need(dve, xn_ready, t)
                nc.vector.reciprocal(rstd[:, :], std[:, :]).then_inc(ln_v, 1)
                dve.wait_ge(ln_v, t * LN + LN)
                nc.vector.scalar_tensor_tensor(offset[:, :], mean[:, :], -1.0, rstd[:, :],
                                               ALU.mult, ALU.mult).then_inc(scale_v, 1)

            def bias_values(t, b, g):
                v = 2 * t + g
                dve.wait_ge(qkv_ready, t * C + g * CU + CU)
                part = qkv[b][:, g * CU:g * CU + CU, 2 * E:3 * E]
                nc.vector.tensor_tensor(part, part, bqkv[:, 2 * E:3 * E].unsqueeze(1).to_broadcast([P, CU, E]),
                                        ALU.add).then_inc(v_ready, 1)

            def row_max(t, g):
                v = 2 * t + g
                dve.wait_ge(qk_summed, CU * v + CU)
                rows = score[g].rearrange("p c (q k) -> p (c q) k", q=H)
                nc.vector.tensor_reduce(top[:, :], rows, AX.X, ALU.max).then_inc(top_v, 1)
                dve.wait_ge(top_v, v + 1)
                nc.vector.tensor_tensor(less[:, :, :].rearrange("p c (q k) -> p (c q) k", q=H), rows,
                                        top[:, :].unsqueeze(2).to_broadcast([P, CU * H, H]),
                                        ALU.subtract).then_inc(less_v, 1)

            def row_sum(t, g):
                v = 2 * t + g
                dve.wait_ge(prob_a, 2 * v + 2)
                nc.vector.tensor_reduce(total[:, 0:DVE_PV * H],
                                        score[g][:, 0:DVE_PV, :].rearrange("p c (q k) -> p (c q) k", q=H),
                                        AX.X, ALU.add)
                nc.vector.tensor_reduce(total[:, DVE_PV * H:CU * H],
                                        prob_sb[g][:, :].rearrange("p (q k) -> p q k", q=H),
                                        AX.X, ALU.add).then_inc(total_v, 1)

            def values(t, b, g):
                v = 2 * t + g

                def product(j):
                    c = g * CU + j
                    pr = score[g][:, j, :].rearrange("p (q k) -> p q k", q=H)
                    dve.wait_ge(v_ready, v + 1)
                    val = qkv[b][:, c, 2 * E:3 * E].rearrange("p (k d) -> p d k", k=H)
                    nc.vector.tensor_tensor(pv_dve[j][:, :, :, :],
                                            pr.unsqueeze(2).to_broadcast([P, H, D, H]),
                                            val.unsqueeze(1).to_broadcast([P, H, D, H]),
                                            ALU.mult).then_inc(pv_mult_v, 1)

                def reduction(j):
                    dve.wait_ge(pv_mult_v, DVE_PV * v + j + 1)
                    nc.vector.tensor_reduce(sums[:, j, :].rearrange("p (q d) -> p q d", q=H), pv_dve[j][:, :, :, :],
                                            AX.X, ALU.add).then_inc(pv_sum_v, 1)

                product(0)
                for j in range(1, DVE_PV):
                    product(j)
                    reduction(j - 1)
                    if j == 1:
                        dve.wait_ge(total_v, v + 1)
                        nc.vector.reciprocal(recip[:, :], total[:, :]).then_inc(recip_v, 1)
                reduction(DVE_PV - 1)

            def divide(t, b, g, full):
                v = 2 * t + g
                need(dve, stored[b], full)
                dve.wait_ge(pv_sum_v, DVE_PV * v + DVE_PV)
                dve.wait_ge(recip_v, v + 1)
                r = recip[:, :].rearrange("p (c q) -> p c q", c=CU).unsqueeze(3).to_broadcast([P, CU, H, D])
                o = out[b][:, :, g * CU:g * CU + CU, :].rearrange("p q c d -> p c q d")
                nc.vector.tensor_tensor(o[:, 0:DVE_PV], sums[:, :, :].rearrange("p c (q d) -> p c q d", q=H),
                                        r[:, 0:DVE_PV], ALU.mult)
                dve.wait_ge(pv_summed, v + 1)
                nc.vector.tensor_tensor(o[:, DVE_PV], o_acc.rearrange("p (q d) -> p q d", q=H), r[:, DVE_PV],
                                        ALU.mult).then_inc(norm_v, 1)

            def batch(t, b, more=True, far=True, i=None):
                i = t // 2 if isinstance(t, int) else i
                row_max(t, 0)
                if isinstance(t, int) and t == 0:
                    pass
                elif b == 1:
                    divide(t - 1, 0, 1, 16 * i)
                else:
                    divide(t - 1, 1, 1, 16 * i - 16)
                row_sum(t, 0)
                values(t, b, 0)
                bias_values(t, b, 1)
                row_max(t, 1)
                if far:
                    statistics(t + 2, b, 16 * i + 32)
                divide(t, b, 0, 16 * i)
                row_sum(t, 1)
                if far:
                    scales(t + 2, b)
                values(t, b, 1)
                if more:
                    bias_values(t + 1, 1 - b, 0)

            statistics(0, 0, 16)
            dve.wait_ge(mod_mm, 1)
            nc.vector.tensor_copy(raw[:, :, :], t_acc[:, 0:6 * NB].rearrange("p (j n) -> p j n", j=6)).then_inc(silu_v, 1)
            dve.wait_ge(silu_v, 4)
            nc.vector.tensor_copy(mod[:, 0:6:3, :], raw[:, 0:6:3, :]).then_inc(mod_v, 1)
            nc.vector.tensor_scalar(mod[:, 1:6:3, :], raw[:, 1:6:3, :], 1.0, None, ALU.add).then_inc(mod_v, 1)
            nc.vector.tensor_scalar(sgn[:, :, :], raw[:, 2:6:3, :], 0.0, 2.0, ALU.is_ge, ALU.mult).then_inc(mod_v, 1)
            nc.vector.scalar_tensor_tensor(mag[:, :, :], raw[:, 2:6:3, :], -1.0, raw[:, 2:6:3, :],
                                           ALU.mult, ALU.max).then_inc(mod_v, 1)
            dve.wait_ge(mod_v, 4)
            nc.vector.tensor_scalar(mag[:, :, :], mag[:, :, :], 0.25, None, ALU.max).then_inc(mod_v, 1)
            dve.wait_ge(mod_v, 5)
            nc.vector.scalar_tensor_tensor(mod[:, 2:6:3, :], sgn[:, :, :], -1.0, mag[:, :, :],
                                           ALU.add, ALU.mult).then_inc(mod_v, 1)
            scales(0, 0)
            dve.wait_ge(mod_tr, 1)
            nc.vector.tensor_copy(modT[:, :], ps[0:4 * NB, 7, 0:E]).then_inc(modT_v, 1)
            statistics(1, 1, 16)
            scales(1, 1)
            bias_values(0, 0, 0)
            for b in range(2):
                batch(b, b)
            with dve.Fori(1, NB // 2 - 1) as i:
                for b in range(2):
                    batch(2 * i + b, b, i=i)
            for b in range(2):
                batch(NB - 2 + b, b, more=b == 0, far=False)
            divide(NB - 1, 1, 1, NB // 2 * 16 - 16)

        @block.tensor
        def _(pe):
            pe.wait_ge(wmod_in, 16)
            pe.wait_ge(silu_v, 3)
            for j in range(6):
                last = nc.tensor.matmul(t_acc[:, j * NB:j * NB + NB], wmod[:, j, :], silu[:, :], start=True, stop=True)
            last.then_inc(mod_mm, 1)
            pe.wait_ge(silu_v, 4)

            def turn(t, b):
                for r in range(2):
                    pe.wait_ge(xn_ready, t + 1)
                    need(pe, hT_done, 2 * t + r)
                    for j in range(CU):
                        last = nc.tensor.transpose(t_acc[:, j * P:j * P + P], x[b][:, r * CU + j, :], ident[:, :])
                    last.then_inc(xt_mm, 1)

            def project(t, cs):
                for c in cs:
                    k = t * C + c
                    if c % CU == 0:
                        pe.wait_ge(hT_done, 2 * t + c // CU + 1)
                    need(pe, qkv_copied, k - 1)
                    nc.tensor.matmul(q_acc[c % 2], hT[:, c * P:c * P + P], wqkv[:, :],
                                     start=True, stop=True).then_inc(qkv_mm, 1)

            def sum_scores(t, b, g, js):
                v = 2 * t + g
                need(pe, pv_mult_v, DVE_PV * (v - 1))
                for j in js:
                    c = g * CU + j
                    pe.wait_ge(qk_prod_ready, CU * v + j + 1)
                    for d in range(D):
                        last = nc.tensor.matmul(score[g][:, j, :], ident[:, :],
                                                flat(qk_prod[c % QK_RING][:, d, :, :]), start=d == 0, stop=d == D - 1)
                    last.then_inc(qk_summed, 1)

            def sum_values(t, g):
                v = 2 * t + g
                pe.wait_ge(pv_prod_ready, v + 1)
                need(pe, norm_v, v)
                for k in range(H):
                    last = nc.tensor.matmul(o_acc, ident[:, :], flat(pv_pool[:, k, :, :]),
                                            start=k == 0, stop=k == H - 1)
                last.then_inc(pv_summed, 1)

            def batch(t, b, more=True):
                if more:
                    turn(t + 1, 1 - b)
                sum_scores(t, b, 1, range(2))
                if more:
                    project(t + 1, range(2))
                sum_scores(t, b, 1, range(2, CU))
                sum_values(t, 0)
                if more:
                    project(t + 1, range(2, CU + 1))
                    for j in range(CU):
                        sum_scores(t + 1, 1 - b, 0, range(j, j + 1))
                        if j != 2:
                            k = CU + 1 + j - (j > 2)
                            project(t + 1, range(k, k + 1))
                sum_values(t, 1)

            pe.wait_ge(mod_v, 6)
            nc.tensor.transpose(ps[0:4 * NB, 7, 0:E], flat(mod[:, 2:6, :]), ident[:, :]).then_inc(mod_tr, 1)
            turn(0, 0)
            project(0, range(C))
            sum_scores(0, 0, 0, range(CU))
            steps(pe, batch)


def merge(nc, io, scr, keep, mod, ident, ps):
    x1, h2T, h2_rows, rows, logits, bog, wog = (
        keep[k] for k in ("x1", "h2T", "h2_rows", "rows", "logits", "bo_gated", "wo_gated"))
    with ExitStack() as ctx:
        sb = lambda n, s, d=F32: ctx.enter_context(nc.sbuf_tensor("merge_" + n, s, d))
        sem = lambda n: ctx.enter_context(nc.semaphore("merge_" + n))
        gw = sb("gate_w", [P, NX])
        o = [sb(f"o{b}", [P, C, E]) for b in range(2)]
        x = [sb(f"x_in{b}", [P, C, E]) for b in range(2)]
        xb = [sb(f"x_biased{b}", [P, C, E]) for b in range(2)]
        attn, xn = sb("attnT", [P, S]), [sb(f"xn{b}", [P, C, E]) for b in range(2)]
        h2 = [sb(f"h2T{b}", [P, S]) for b in range(2)]
        scaled = sb("scaled", [P, C, E])
        now = [sb(f"now{b}", [P, 2, 1]) for b in range(2)]
        stats, mean, var = sb("stats", [P, C, 6]), sb("mean", [P, C]), sb("var", [P, C])
        tmp = [sb(f"moment_tmp{k}", [P, C])[:, :] for k in range(3)]
        std, rstd = sb("std", [P, C]), sb("rstd", [P, C])
        w_in, consts_in, seen = sem("w_in"), sem("consts_in"), sem("waits_seen")
        o_in = [sem(f"o_in{b}") for b in range(2)]
        x_in = [sem(f"x_in{b}") for b in range(2)]
        o_tr, attn_a, xb_p, proj_mm = sem("o_tr"), sem("attn_a"), sem("x_biased_p"), sem("proj_mm")
        x1_v, ln_v, var_v, std_a, xn_v, xn_tr, h2_a = (
            sem("x1_v"), sem("ln_v"), sem("var_v"), sem("std_a"), sem("xn_v"), sem("xn_tr"), sem("h2_a"))
        scaled_p, h2_rows_p = sem("scaled_p"), sem("h2_rows_p")
        logit_mm, logit_v = sem("logit_mm"), sem("logit_v")
        h2_kept = [sem(f"h2_kept{b}") for b in range(2)]
        pA, pB, pC = (flat(ps[:, 2 * j:2 * j + 2, :]) for j in range(3))
        pD = ps[:, 6, 0:C * NX]
        x_dram = io["x"].rearrange("n (p c) e -> n p c e", c=C)
        o_dram = scr["o"].rearrange("n h (r c e) -> n (h r) c e", c=C, e=E)
        block = ctx.enter_context(nc.Block())

        def steps(engine, first, second):
            def one(n, b, i, before):
                first(n, b, i)
                if before:
                    second(*before)

            one(0, 0, 0, None)
            one(1, 1, 0, (0, 0, 0))
            with engine.Fori(1, NB // 2) as i:
                one(2 * i, 0, i, (2 * i - 1, 1, i - 1))
                one(2 * i + 1, 1, i, (2 * i, 0, i))
            second(NB - 1, 1, NB // 2 - 1)

        def steps_ahead(engine, first, ahead, second, last=None):
            def one(n, b, i, before, after):
                if first:
                    first(n, b)
                if after:
                    ahead(*after)
                if before:
                    second(*before)
                if last:
                    last(n)

            ahead(0, 0, 0)
            one(0, 0, 0, None, (1, 1, 0))
            one(1, 1, 0, (0, 0, 0), (2, 0, 1))
            with engine.Fori(1, NB // 2 - 1) as i:
                one(2 * i, 0, i, (2 * i - 1, 1, i - 1), (2 * i + 1, 1, i))
                one(2 * i + 1, 1, i, (2 * i, 0, i), (2 * i + 2, 0, i + 1))
            i = NB // 2 - 1
            one(2 * i, 0, i, (2 * i - 1, 1, i - 1), (2 * i + 1, 1, i))
            one(2 * i + 1, 1, i, (2 * i, 0, i), None)
            second(NB - 1, 1, i)

        @block.sync
        def _(sp):

            def load(n, b):
                sp.dma_start(o[b][:, :, :], o_dram[n]).then_inc(o_in[b], 16)
                sp.dma_start(x[b][:, :, :], x_dram[n]).then_inc(x_in[b], 16)

            def store(n, b):
                sp.wait_ge(h2_a, n + 1)
                sp.dma_start(h2T[:, bass.ds(n, 1), :].rearrange("p o s -> p (o s)"), h2[b][:, :]).then_inc(h2_kept[b], 16)

            load(0, 0)
            sp.dma_start(gw[:, :], io["gate_w"]).then_inc(w_in, 16)
            load(1, 1)
            for name in ("gate_b", "rank", "block_starts", "block_numbers"):
                sp.dma_start(keep[name][:, :], io[name].partition_broadcast(P)).then_inc(consts_in, 16)
            for name, source in (("upper", "upper"), ("ids", "token_ids")):
                sp.dma_start(keep[name][:, :], io[source]).then_inc(consts_in, 16)
            for n in range(2):
                sp.wait_ge(x1_v, n + 1)
                load(n + 2, n)
            store(0, 0)
            with sp.Fori(1, NB // 2 - 1) as i:
                for b in range(2):
                    n = 2 * i + b
                    sp.wait_ge(x1_v, n + 1)
                    load(n + 2, b)
                    store(n - 1, 1 - b)
            for n in range(NB - 3, NB):
                store(n, n % 2)
            for b in range(2):
                sp.wait_ge(h2_kept[b], 16 * (NB // 2))
            sp.wait_ge(consts_in, 96)

        @block.gpsimd
        def _(pool):
            def first(n, b, i):
                pool.wait_ge(x_in[b], 16 * i + 16)
                need(pool, x1_v, n - 1)
                pool.sem_inc(seen, 1)
                nc.gpsimd.tensor_tensor(xb[b][:, :, :], x[b][:, :, :],
                                        bog[:, bass.ds(n, 1), :].to_broadcast([P, C, E]), ALU.add).then_inc(xb_p, 1)

            def second(n, b, i):
                pool.wait_ge(xn_v, n + 1)
                need(pool, h2_rows_p, n)
                pool.sem_inc(seen, 1)
                nc.gpsimd.tensor_tensor(scaled[:, :, :], xn[b][:, :, :],
                                        rows[:, 2, bass.ds(n, 1), :].to_broadcast([P, C, E]), ALU.mult).then_inc(scaled_p, 1)
                pool.wait_ge(scaled_p, n + 1)
                pool.sem_inc(seen, 1)
                nc.gpsimd.tensor_tensor(h2_rows[:, bass.ds(n * C, C), 0:E], scaled[:, :, :],
                                        rows[:, 1, bass.ds(n, 1), :].to_broadcast([P, C, E]), ALU.add).then_inc(h2_rows_p, 1)

            steps(pool, first, second)

        @block.vector
        def _(dve):
            def first(n, b, i):
                dve.wait_ge(xb_p, n + 1)
                dve.wait_ge(proj_mm, n + 1)
                nc.vector.tensor_tensor(x1[:, bass.ds(n, 1), :, :].rearrange("p o c e -> p (o c e)"), pB,
                                        flat(xb[b][:, :, :]), ALU.add).then_inc(x1_v, 1)
                dve.wait_ge(x1_v, n + 1)
                need(dve, h2_a, n - 1)
                nc.vector.tensor_scalar(now[b][:, :, :], mod[:, 3:5, bass.ds(n, 1)], 1.0, None, ALU.mult)
                base = n * (C + 3)
                for c in range(C):
                    nc.vector.bn_stats(stats[:, c, :],
                                       x1[:, bass.ds(n, 1), c, :].rearrange("p o e -> p (o e)")).then_inc(ln_v, 1)
                moments(nc, dve, stats, mean[:, :], tmp, var[:, :], ln_v, base + C, var_v)
                dve.wait_ge(std_a, n + 1)
                nc.vector.reciprocal(rstd[:, :], std[:, :]).then_inc(ln_v, 1)
                need(dve, h2_rows_p, n - 1)
                need(dve, xn_tr, n - 1)
                dve.wait_ge(ln_v, base + C + 3)
                for c in range(C):
                    last = nc.vector.tensor_scalar(xn[b][:, c, :],
                                                   x1[:, bass.ds(n, 1), c, :].rearrange("p o e -> p (o e)"),
                                                   mean[:, c:c + 1], rstd[:, c:c + 1], ALU.subtract, ALU.mult)
                last.then_inc(xn_v, 1)

            def second(n, b, i):
                dve.wait_ge(logit_mm, n + 1)
                nc.vector.tensor_scalar(logits[:, bass.ds(n, 1), :, :].rearrange("p o c e -> p (o c e)"),
                                        pD, 1.0, None, ALU.mult).then_inc(logit_v, 1)

            steps(dve, first, second)

        @block.scalar
        def _(act):
            def ahead(n, b, i):
                act.wait_ge(o_tr, n + 1)
                need(act, proj_mm, n)
                nc.scalar.activation(attn[:, :], pA, ACT.Identity).then_inc(attn_a, 1)

            def second(n, b, i):
                act.wait_ge(xn_tr, n + 1)
                need(act, logit_mm, n - 1)
                need(act, h2_kept[b], 16 * i)
                nc.scalar.activation(h2[b][:, :], pC, ACT.Identity, bias=now[b][:, 0, :],
                                     scale=now[b][:, 1, :]).then_inc(h2_a, 1)

            def deviation(n):
                act.wait_ge(var_v, n + 1)
                nc.scalar.activation(std[:, :], var[:, :], ACT.Sqrt).then_inc(std_a, 1)

            steps_ahead(act, None, ahead, second, deviation)

        @block.tensor
        def _(pe):
            pe.wait_ge(w_in, 16)

            def ahead(n, b, i):
                pe.wait_ge(o_in[b], 16 * i + 16)
                need(pe, attn_a, n)
                for c in range(C):
                    last = nc.tensor.transpose(pA[:, c * P:c * P + P], o[b][:, c, :], ident[:, :])
                last.then_inc(o_tr, 1)

            def first(n, b):
                need(pe, x1_v, n)
                pe.wait_ge(attn_a, n + 1)
                for c in range(C):
                    last = nc.tensor.matmul(pB[:, c * P:c * P + P], attn[:, c * P:c * P + P], wog[:, bass.ds(n, 1), :].rearrange("p o e -> p (o e)"),
                                            start=True, stop=True)
                last.then_inc(proj_mm, 1)

            def second(n, b, i):
                need(pe, h2_a, n)
                pe.wait_ge(xn_v, n + 1)
                for c in range(C):
                    last = nc.tensor.transpose(pC[:, c * P:c * P + P], xn[b][:, c, :], ident[:, :])
                last.then_inc(xn_tr, 1)
                need(pe, logit_v, n)
                pe.wait_ge(h2_a, n + 1)
                for c in range(C):
                    last = nc.tensor.matmul(pD[:, c * NX:c * NX + NX], h2[b][:, c * P:c * P + P], gw[:, :],
                                            start=True, stop=True)
                last.then_inc(logit_mm, 1)

            steps_ahead(pe, first, ahead, second)


def load_expert(sp, io, keep, e, b, parts, w1_in, w2_in):
    if 1 in parts:
        sp.dma_start(keep["w1"][b][:, :], io["w1"][bass.ds(e, 1)].rearrange("o p k -> p (o k)")).then_inc(w1_in, 16)
    if 2 in parts:
        sp.dma_start(keep["w2"][b][:, :], io["w2_pack"][bass.ds(e, 1)].rearrange("o p k -> p (o k)")
                     ).then_inc(w2_in, 16)
        sp.dma_start(keep["b2"][b][:, :], io["b2"][bass.ds(e, 1)].rearrange("o k -> (o k)").partition_broadcast(P)
                     ).then_inc(w2_in, 16)


def dispatch(nc, io, scr, keep, ps):
    x1, h2T, h2_rows, rows, weight, slot, ids, logits, block_expert = (
        keep[k] for k in ("x1", "h2T", "h2_rows", "rows", "weight", "slot", "ids", "logits", "block_expert"))
    gb, rank, steps_of, block_no, upper = (
        keep[k] for k in ("gate_b", "rank", "block_starts", "block_numbers", "upper"))
    T, Q = NB * C, BT // P
    with ExitStack() as ctx:
        sb = lambda n, s, d=F32: ctx.enter_context(nc.sbuf_tensor("dispatch_" + n, s, d))
        sem = lambda n: ctx.enter_context(nc.semaphore("dispatch_" + n))
        w1, w2, b1, b2 = sb("w1", [P, HID]), sb("w2", [P, HC, E]), sb("b1", [P, HC]), sb("b2_rows", [P, E])
        hid = [sb(f"hid{b}", [P, HC, BT]) for b in range(2)]
        part = [sb(f"part{b}", [P, Q, E]) for b in range(2)]
        ones = sb("ones", [P, P])
        lg = sb("lg", [P, T, NX])
        pick = [sb(f"pick{k}", [P, T, NX]) for k in range(2)]
        work = sb("work", [P, T, NX])
        top = [sb(f"top{k}", [P, T]) for k in range(2)]
        first, gap = sb("first", [P, T]), sb("gap", [P, T])
        taken = sb("taken", [P, NX, T])
        scan = [sb(f"scan{k}", [P, NX, T]) for k in range(2)]
        total = sb("total", [P, NX])
        count, over = sb("count", [P, NX]), sb("over", [P, NX, S * NB // BT])
        ends = [sb(f"ends{k}", [P, NX]) for k in range(4)]
        base, past, slot_f = sb("base", [P, NX]), sb("past", [P, BLOCKS, NX]), sb("slot_f", [P, T])
        expert_f = sb("expert_f", [P, BLOCKS])
        w_in, up_mm, gelu_a, down_mm, biased_v, gated_v, x1_v = (
            sem("w_in"), sem("up_mm"), sem("gelu_a"), sem("down_mm"), sem("biased_v"), sem("gated_v"), sem("x1_v"))
        sent = [sem(f"rows_sent{k}") for k in range(2)]
        second_v, slot_v, block_v, ahead_in = sem("second_choice_v"), sem("slot_v"), sem("block_v"), sem("ahead_in")
        v, gap_v, exp_a, total_v, count_mm = sem("v"), sem("gap_v"), sem("gap_exp"), sem("total_v"), sem("count_mm")
        up = [ps[:, j, :] for j in range(HC)]
        down = [ps[:, 4 + b, :] for b in range(2)]
        before, counts = ps[:, 6, 0:NX], ps[:, 7, 0:NX]
        block = ctx.enter_context(nc.Block())

        @block.sync
        def _(sp):
            sp.dma_start(w1[:, :], io["ws1"]).then_inc(w_in, 16)
            sp.dma_start(w2[:, :, :], io["ws2"].rearrange("(c p) d -> p c d", p=P)).then_inc(w_in, 16)
            sp.dma_start(b1[:, :], io["bs1T"]).then_inc(w_in, 16)
            sp.dma_start(b2[:, :], io["bs2"].partition_broadcast(P)).then_inc(w_in, 16)
            sp.dma_start(keep["spare_rows"][:, :], io["spare_rows"]).then_inc(ahead_in, 16)
            sp.wait_ge(block_v, 1)
            for b in range(RING):
                e = sp.value_load(block_expert[0:1, b:b + 1], min_val=0, max_val=NX - 1)
                load_expert(sp, io, keep, e, b, (1, 2), ahead_in, ahead_in)
            sp.wait_ge(ahead_in, 16 + 48 * RING)

        @block.gpsimd
        def _(pool):
            pool.wait_ge(slot_v, 1)
            for k in range(2):
                if k:
                    pool.wait_ge(second_v, 2)
                for t in range(T):
                    nc.gpsimd.indirect_dma_start(
                        scr["slots"], bass.IndirectOffsetOnAxis(ap=slot[:, k, t:t + 1], axis=0),
                        h2_rows[:, t, :], None).then_inc(sent[k], 16)
            pool.wait_ge(sent[1], 16 * T)

        @block.tensor
        def _(pe):
            def ups(n, b):
                k = 2 * n + b
                for j in range(HC):
                    need(pe, gelu_a, (k - 1) * HC + j + 1)
                    nc.tensor.matmul(up[j], w1[:, j * P:j * P + P],
                                     h2T[:, bass.ds(n, 1), b * BT:b * BT + BT].rearrange("p o s -> p (o s)"),
                                     start=True, stop=True).then_inc(up_mm, 1)

            def downs(n, b):
                k = 2 * n + b
                need(pe, biased_v, k - 1)
                pe.wait_ge(gelu_a, k * HC + HC)
                for q in range(Q):
                    for j in range(HC):
                        last = nc.tensor.matmul(down[b][:, q * E:q * E + E], hid[b][:, j, q * P:q * P + P],
                                                w2[:, j, :], start=j == 0, stop=j == HC - 1)
                last.then_inc(down_mm, 1)

            pe.wait_ge(w_in, 64)
            ups(0, 0)
            pe.wait_ge(total_v, 1)
            nc.tensor.matmul(before, upper[:, :], total[:, :], start=True, stop=True)
            nc.tensor.matmul(counts, ones[:, :], total[:, :], start=True, stop=True).then_inc(count_mm, 1)
            ups(0, 1)
            downs(0, 0)
            with pe.Fori(1, NB) as n:
                ups(n, 0)
                downs(n - 1, 1)
                ups(n, 1)
                downs(n, 0)
            downs(NB - 1, 1)

        @block.scalar
        def _(act):
            act.wait_ge(gap_v, 1)
            nc.scalar.activation(gap[:, :], gap[:, :], ACT.Exp).then_inc(exp_a, 1)
            act.wait_ge(w_in, 64)

            def gelus(n, b):
                k = 2 * n + b
                need(act, down_mm, k - 1)
                for j in range(HC):
                    act.wait_ge(up_mm, k * HC + j + 1)
                    nc.scalar.activation(hid[b][:, j, :], up[j], ACT.Gelu, bias=b1[:, j:j + 1]).then_inc(gelu_a, 1)

            for b in range(2):
                gelus(0, b)
            with act.Fori(1, NB) as n:
                for b in range(2):
                    gelus(n, b)

        @block.vector
        def _(dve):
            def add(n, b):
                k = 2 * n + b
                here = x1[:, bass.ds(n, 1), b * Q:b * Q + Q, :].rearrange("p o c e -> p (o c) e")
                need(dve, x1_v, k - 1)
                dve.wait_ge(down_mm, k + 1)
                nc.vector.tensor_tensor(part[b][:, :, :], down[b].rearrange("p (q e) -> p q e", q=Q),
                                        b2[:, :].unsqueeze(1).to_broadcast([P, Q, E]), ALU.add).then_inc(biased_v, 1)
                dve.wait_ge(biased_v, k + 1)
                nc.vector.tensor_tensor(part[b][:, :, :], part[b][:, :, :],
                                        rows[:, 3, bass.ds(n, 1), :].to_broadcast([P, Q, E]), ALU.mult).then_inc(gated_v, 1)
                dve.wait_ge(gated_v, k + 1)
                nc.vector.tensor_tensor(here, here, part[b][:, :, :], ALU.add).then_inc(x1_v, 1)

            done = [0]

            def step(instruction):
                done[0] += 1
                instruction.then_inc(v, 1)
                dve.wait_ge(v, done[0])

            tt, ts = nc.vector.tensor_tensor, nc.vector.tensor_scalar
            over_t = lambda ap: ap.unsqueeze(1).to_broadcast([P, T, NX])
            over_e = lambda ap: ap.unsqueeze(2).to_broadcast([P, T, NX])
            nc.vector.memset(ones[:, :], 1.0)
            step(tt(lg[:, :, :], logits[:, :, :, :].rearrange("p n c e -> p (n c) e"), over_t(gb[:, :]), ALU.add))
            for k in range(2):
                step(nc.vector.tensor_reduce(top[k][:, :], lg[:, :, :], AX.X, ALU.max))
                step(tt(work[:, :, :], lg[:, :, :], over_e(top[k][:, :]), ALU.is_ge))
                step(tt(work[:, :, :], work[:, :, :], over_t(rank[:, :]), ALU.mult))
                step(nc.vector.tensor_reduce(first[:, :], work[:, :, :], AX.X, ALU.max))
                step(tt(pick[k][:, :, :], work[:, :, :], over_e(first[:, :]), ALU.is_equal))
                if k == 0:
                    step(nc.vector.scalar_tensor_tensor(lg[:, :, :], pick[0][:, :, :], -3.0e38, lg[:, :, :],
                                                        ALU.mult, ALU.add))
            tt(gap[:, :], top[1][:, :], top[0][:, :], ALU.subtract).then_inc(gap_v, 1)
            by_expert = lambda ap: ap.rearrange("p t e -> p e t")
            step(tt(taken[:, :, :], by_expert(pick[0][:, :, :]), by_expert(pick[1][:, :, :]), ALU.add))
            now = taken
            for k in range(6):
                d, new = 2 ** k, scan[k % 2]
                nc.vector.tensor_copy(new[:, :, 0:d], now[:, :, 0:d])
                step(tt(new[:, :, d:T], now[:, :, d:T], now[:, :, 0:T - d], ALU.add))
                now = new
            nc.vector.tensor_copy(total[:, :], now[:, :, T - 1]).then_inc(total_v, 1)
            step(tt(scan[0][:, :, :], now[:, :, :], taken[:, :, :], ALU.subtract))
            now = scan[0]
            dve.wait_ge(exp_a, 1)
            step(ts(weight[:, 0, :], gap[:, :], 1.0, None, ALU.add))
            step(nc.vector.reciprocal(weight[:, 0, :], weight[:, 0, :]))
            step(tt(weight[:, 1, :], weight[:, 0, :], gap[:, :], ALU.mult))
            dve.wait_ge(count_mm, 1)
            step(nc.vector.tensor_copy(count[:, :], counts))
            m = S * NB // BT
            step(tt(over[:, :, :], count[:, :].unsqueeze(2).to_broadcast([P, NX, m]),
                    steps_of[:, :].unsqueeze(1).to_broadcast([P, NX, m]), ALU.is_gt))
            step(nc.vector.tensor_reduce(ends[0][:, :], over[:, :, :], AX.X, ALU.add))
            for k in range(3):
                d = 2 ** k
                nc.vector.tensor_copy(ends[k + 1][:, 0:d], ends[k][:, 0:d])
                step(tt(ends[k + 1][:, d:NX], ends[k][:, d:NX], ends[k][:, 0:NX - d], ALU.add))
            step(tt(base[:, :], ends[3][:, :], ends[0][:, :], ALU.subtract))
            step(ts(base[:, :], base[:, :], float(BT), None, ALU.mult))
            step(tt(base[:, :], base[:, :], before, ALU.add))
            step(tt(now[:, :, :], now[:, :, :], base[:, :].unsqueeze(2).to_broadcast([P, NX, T]), ALU.add))
            def slots_of(k):
                step(tt(work[:, :, :], pick[k][:, :, :], now[:, :, :].rearrange("p e t -> p t e"), ALU.mult))
                step(nc.vector.tensor_reduce(slot_f[:, :], work[:, :, :], AX.X, ALU.add))
                return nc.vector.tensor_copy(slot[:, k, :], slot_f[:, :])

            nc.vector.tensor_copy(h2_rows[:, :, E], ids[:, :])
            nc.vector.tensor_copy(h2_rows[:, :, E + 1], weight[:, 0, :])
            slots_of(0).then_inc(slot_v, 1)
            dve.wait_ge(slot_v, 1)
            step(slots_of(1))
            step(tt(past[:, :, :], block_no[:, :].unsqueeze(2).to_broadcast([P, BLOCKS, NX]),
                    ends[3][:, :].unsqueeze(1).to_broadcast([P, BLOCKS, NX]), ALU.is_ge))
            step(nc.vector.tensor_reduce(expert_f[:, :], past[:, :, :], AX.X, ALU.add))
            step(ts(expert_f[:, :], expert_f[:, :], float(NX - 1), None, ALU.min))
            nc.vector.tensor_copy(block_expert[:, :], expert_f[:, :]).then_inc(block_v, 1)
            dve.wait_ge(w_in, 64)
            for b in range(2):
                add(0, b)
            with dve.Fori(1, NB // 2) as n:
                for b in range(2):
                    add(n, b)
            dve.wait_ge(sent[0], 16 * T)
            nc.vector.tensor_scalar(h2_rows[:, :, E], ids[:, :], float(NB * S), None, ALU.add).then_inc(second_v, 1)
            nc.vector.tensor_copy(h2_rows[:, :, E + 1], weight[:, 1, :]).then_inc(second_v, 1)
            with dve.Fori(NB // 2, NB) as n:
                for b in range(2):
                    add(n, b)


def experts(nc, io, scr, keep, ident, ps):
    block_expert = keep["block_expert"]
    Q, TURNS = BT // P, BLOCKS // RING
    w1, w2, b2, spare = (keep[k] for k in ("w1", "w2", "b2", "spare_rows"))
    with ExitStack() as ctx:
        sb = lambda n, s, d=F32: ctx.enter_context(nc.sbuf_tensor("expert_" + n, s, d))
        sem = lambda n: ctx.enter_context(nc.semaphore("expert_" + n))
        x = [sb(f"x{b}", [P, Q, E + 2]) for b in range(RING)]
        x_high, x_low, w_high, w_low = (
            [sb(f"{n}{b}", [P, BT], F32R) for b in range(RING)] for n in ("x_high", "x_low", "w1_high", "w1_low"))
        hid = [sb(f"hid{b}", [P, HC, BT]) for b in range(RING)]
        biased = [sb(f"biased{b}", [P, Q, E]) for b in range(RING)]
        y = [sb(f"y{b}", [P, Q, E]) for b in range(RING)]
        empty = [sb(f"empty{b}", [P, Q]) for b in range(RING)]
        target = [sb(f"target{b}", [P, Q]) for b in range(RING)]
        row = [sb(f"row{b}", [P, Q], I32) for b in range(RING)]
        weight = [sb(f"weight{b}", [P, Q]) for b in range(RING)]
        w1_in = [sem(f"w1_in{b}") for b in range(RING)]
        w2_in = [sem(f"w2_in{b}") for b in range(RING)]
        x_in = [sem(f"x_in{b}") for b in range(RING)]
        x_tr, x_high_v, xT_v, w_high_a, w_low_v, up_mm, gelu_a, down_mm, empty_v, target_v, biased_v, y_v = (
            sem("x_tr"), sem("x_high_v"), sem("xT_v"), sem("w_high_a"), sem("w_low_v"), sem("up_mm"), sem("gelu_a"), sem("down_mm"),
            sem("empty_v"), sem("target_v"), sem("biased_v"), sem("y_v"))
        y_sent, y_seen = [sem(f"y_sent{b}") for b in range(RING)], sem("y_seen")
        up = [ps[:, j, :] for j in range(HC)]
        down = [ps[:, 4 + b, :] for b in range(RING)]
        tr = ps[:, 7, :]
        slots = scr["slots"].rearrange("(m p q) e -> m p q e", p=P, q=Q)
        block = ctx.enter_context(nc.Block())

        @block.sync
        def _(sp):
            def load_x(m, b):
                sp.dma_start(x[b][:, :, :], slots[m]).then_inc(x_in[b], 16)

            def expert(m):
                return sp.value_load(block_expert[0:1, bass.ds(m, 1)], min_val=0, max_val=NX - 1)

            for b in range(RING):
                load_x(b, b)

            def ahead(m, b):
                e1, e2 = expert(m + RING), expert(m + RING - 1)
                sp.wait_ge(w_low_v, m + 1)
                load_expert(sp, io, keep, e1, b, (1,), w1_in[b], None)
                sp.wait_ge(target_v, m + 1)
                load_x(m + RING, b)
                if not isinstance(m, int) or m > 0:
                    sp.wait_ge(biased_v, m)
                    c = (b - 1) % RING
                    load_expert(sp, io, keep, e2, c, (2,), None, w2_in[c])

            for b in range(RING):
                ahead(b, b)
            with sp.Fori(1, TURNS - 1) as i:
                for b in range(RING):
                    ahead(RING * i + b, b)
            e = expert(BLOCKS - 1)
            sp.wait_ge(biased_v, BLOCKS - RING)
            load_expert(sp, io, keep, e, RING - 1, (2,), None, w2_in[RING - 1])

        def steps(engine, one):
            for b in range(RING):
                one(b, b, 0)
            with engine.Fori(1, TURNS) as i:
                for b in range(RING):
                    one(RING * i + b, b, i)

        @block.gpsimd
        def _(pool):
            def one(m, b, i):
                pool.wait_ge(y_v, m + 1)
                pool.sem_inc(y_seen, 1)
                for q in range(Q):
                    nc.gpsimd.indirect_dma_start(
                        scr["results"], bass.IndirectOffsetOnAxis(ap=row[b][:, q:q + 1], axis=0),
                        y[b][:, q, :], None).then_inc(y_sent[b], 16)

            steps(pool, one)
            for b in range(RING):
                pool.wait_ge(y_sent[b], 16 * Q * TURNS)

        @block.tensor
        def _(pe):
            def turn(m, b, i):
                need(pe, xT_v, m)
                pe.wait_ge(x_in[b], 16 * i + 16)
                for q in range(Q):
                    last = nc.tensor.transpose(tr[:, q * P:q * P + P], x[b][:, q, 0:E], ident[:, :])
                last.then_inc(x_tr, 1)

            def ups(m, b, i):
                pe.wait_ge(w_low_v, m + 1)
                pe.wait_ge(xT_v, m + 1)
                for j in range(HC):
                    need(pe, gelu_a, (m - 1) * HC + j + 1)
                    part = slice(j * P, j * P + P)
                    nc.tensor.matmul(up[j], w_high[b][:, part], x_high[b][:, :], start=True, stop=False)
                    nc.tensor.matmul(up[j], w_high[b][:, part], x_low[b][:, :], start=False, stop=False)
                    nc.tensor.matmul(up[j], w_low[b][:, part], x_high[b][:, :],
                                     start=False, stop=True).then_inc(up_mm, 1)

            def downs(m, b):
                need(pe, biased_v, m - RING + 1)
                pe.wait_ge(gelu_a, m * HC + HC)
                for q in range(Q):
                    for j in range(HC):
                        last = nc.tensor.matmul(down[b][:, q * E:q * E + E], hid[b][:, j, q * P:q * P + P],
                                                w2[b][:, j * E:j * E + E], start=j == 0, stop=j == HC - 1)
                last.then_inc(down_mm, 1)

            def one(m, b, i):
                ups(m, b, i)
                if b < RING - 1:
                    turn(m + 1, b + 1, i)
                elif not isinstance(m, int) or m + 1 < BLOCKS:
                    turn(m + 1, 0, i + 1)
                downs(m - 1, (b - 1) % RING)

            turn(0, 0, 0)
            turn(1, 1, 0)
            ups(0, 0, 0)
            for b in range(1, RING):
                one(b, b, 0)
            with pe.Fori(1, TURNS - 1) as i:
                for b in range(RING):
                    one(RING * i + b, b, i)
            for b in range(RING):
                one(BLOCKS - RING + b, b, TURNS - 1)
            downs(BLOCKS - 1, RING - 1)

        @block.scalar
        def _(act):
            def split(m, b, i):
                need(act, w1_in[b], 16 * i)
                need(act, up_mm, (m - RING + 1) * HC)
                nc.scalar.activation(w_high[b][:, :], w1[b][:, :], ACT.Copy).then_inc(w_high_a, 1)

            def one(m, b, i):
                need(act, w2_in[b], 32 * i)
                need(act, down_mm, m - RING + 1)
                for j in range(HC):
                    act.wait_ge(up_mm, m * HC + j + 1)
                    nc.scalar.activation(hid[b][:, j, :], up[j], ACT.Gelu,
                                         bias=w2[b][:, HID + j:HID + j + 1]).then_inc(gelu_a, 1)
                if not isinstance(m, int) or m + 2 < BLOCKS:
                    split(m + 2, (b + 2) % RING, i if b == 0 else i + 1)

            for b in range(2):
                split(b, b, 0)
            for b in range(RING):
                one(b, b, 0)
            with act.Fori(1, TURNS - 1) as i:
                for b in range(RING):
                    one(RING * i + b, b, i)
            for b in range(RING):
                one(BLOCKS - RING + b, b, TURNS - 1)

        @block.vector
        def _(dve):
            def prepare(m, b, i):
                need(dve, down_mm, m - RING + 1)
                dve.wait_ge(x_tr, m + 1)
                nc.vector.tensor_copy(x_high[b][:, :], tr).then_inc(x_high_v, 1)
                need(dve, up_mm, (m - RING + 1) * HC)
                dve.wait_ge(w_high_a, m + 1)
                nc.vector.tensor_tensor(w_low[b][:, :], w1[b][:, :], w_high[b][:, :], ALU.subtract).then_inc(w_low_v, 1)
                dve.wait_ge(x_high_v, m + 1)
                nc.vector.tensor_tensor(x_low[b][:, :], tr, x_high[b][:, :], ALU.subtract).then_inc(xT_v, 1)
                ids = x[b][:, :, E]
                nc.vector.scalar_tensor_tensor(empty[b][:, :], ids, 0.0, spare[:, bass.ds(m * Q, Q)],
                                               ALU.is_equal, ALU.mult).then_inc(empty_v, 1)
                need(dve, y_v, m - RING + 1)
                nc.vector.tensor_copy(weight[b][:, :], x[b][:, :, E + 1])
                dve.wait_ge(empty_v, m + 1)
                nc.vector.scalar_tensor_tensor(target[b][:, :], ids, -1.0, empty[b][:, :],
                                               ALU.add, ALU.add).then_inc(target_v, 1)

            def finish(m, b, i):
                need(dve, y_v, m - RING + 1)
                dve.wait_ge(down_mm, m + 1)
                nc.vector.tensor_tensor(biased[b][:, :, :], down[b].rearrange("p (q e) -> p q e", q=Q),
                                        b2[b][:, :].unsqueeze(1).to_broadcast([P, Q, E]), ALU.add).then_inc(biased_v, 1)
                dve.wait_ge(target_v, m + 1)
                need(dve, y_sent[b], 16 * Q * i)
                nc.vector.tensor_copy(row[b][:, :], target[b][:, :])
                dve.wait_ge(biased_v, m + 1)
                for q in range(Q):
                    last = nc.vector.tensor_scalar(y[b][:, q, :], biased[b][:, q, :], weight[b][:, q:q + 1], None,
                                                   ALU.mult)
                last.then_inc(y_v, 1)

            def one(m, b, i):
                if b < RING - 1:
                    prepare(m + 1, b + 1, i)
                elif not isinstance(m, int) or m + 1 < BLOCKS:
                    prepare(m + 1, 0, i + 1)
                if not isinstance(m, int) or m > 0:
                    finish(m - 1, (b - 1) % RING, i if b > 0 else i - 1)

            prepare(0, 0, 0)
            for b in range(RING):
                one(b, b, 0)
            with dve.Fori(1, TURNS - 1) as i:
                for b in range(RING):
                    one(RING * i + b, b, i)
            for b in range(RING):
                one(BLOCKS - RING + b, b, TURNS - 1)
            finish(BLOCKS - 1, RING - 1, TURNS - 1)


def combine(nc, io, scr, keep):
    x1, rows, RING = keep["x1"], keep["rows"], 4
    with ExitStack() as ctx:
        sb = lambda n, s, d=F32: ctx.enter_context(nc.sbuf_tensor("combine_" + n, s, d))
        sem = lambda n: ctx.enter_context(nc.semaphore("combine_" + n))
        y = [[sb(f"y{k}_{b}", [P, C, E]) for k in range(2)] for b in range(RING)]
        out = [sb(f"out{b}", [P, C, E]) for b in range(RING)]
        y_in = [sem(f"y_in{b}") for b in range(RING)]
        stored = [sem(f"stored{b}") for b in range(RING)]
        sum_p, gated_v, out_v = sem("sum_p"), sem("gated_v"), sem("out_v")
        results = scr["results"][0:2 * NB * S].rearrange("(k n p c) e -> k n p c e", k=2, n=NB, p=P)
        out_dram = io["out"].rearrange("n (p c) e -> n p c e", c=C)
        block = ctx.enter_context(nc.Block())

        @block.sync
        def _(sp):
            def load(n, b):
                for k in range(2):
                    sp.dma_start(y[b][k][:, :, :], results[k, n]).then_inc(y_in[b], 16)

            for b in range(RING):
                load(b, b)
            for n in range(NB):
                b = n % RING
                if n + RING < NB:
                    sp.wait_ge(sum_p, n + 1)
                    load(n + RING, b)
                sp.wait_ge(out_v, n + 1)
                sp.dma_start(out_dram[n], out[b][:, :, :]).then_inc(stored[b], 16)
            for b in range(RING):
                sp.wait_ge(stored[b], 16 * (NB // RING))

        @block.gpsimd
        def _(pool):
            for n in range(NB):
                b = n % RING
                pool.wait_ge(y_in[b], 32 * (n // RING) + 32)
                need(pool, stored[b], 16 * (n // RING))
                nc.gpsimd.tensor_tensor(out[b][:, :, :], y[b][0][:, :, :], y[b][1][:, :, :], ALU.add).then_inc(sum_p, 1)

        @block.vector
        def _(dve):
            for n in range(NB):
                b = n % RING
                dve.wait_ge(sum_p, n + 1)
                nc.vector.tensor_tensor(out[b][:, :, :], out[b][:, :, :],
                                        rows[:, 3, n:n + 1, :].to_broadcast([P, C, E]), ALU.mult).then_inc(gated_v, 1)
                dve.wait_ge(gated_v, n + 1)
                nc.vector.tensor_tensor(out[b][:, :, :], out[b][:, :, :], x1[:, n, :, :], ALU.add).then_inc(out_v, 1)


def block_kernel(nc, io, out):
    io = dict(io, out=out)
    T = NB * C
    with ExitStack() as ctx:
        sb = lambda n, s, d=F32: ctx.enter_context(nc.sbuf_tensor(n, s, d))
        ps = ctx.enter_context(nc.psum_tensor("ps", [P, 8, 512], F32))
        mod, ident = sb("mod", [P, 6, NB]), sb("ident", [P, P])
        rows = sb("mod_rows", [P, 4, NB, E])
        gated = [sb(f"{n}_gated", [P, NB, E]) for n in ("bo", "wo")]
        ident_in = ctx.enter_context(nc.semaphore("ident_in"))
        scr = {
            "mod": nc.dram_tensor("mod_scratch", [4, NB, E], F32).ap(),
            "o": nc.dram_tensor("o_scratch", [NB, H, S * D], F32).ap(),
            "slots": nc.dram_tensor("slots_scratch", [BLOCKS * BT, E + 2], F32).ap(),
            "results": nc.dram_tensor("results_scratch", [2 * NB * S + BLOCKS * BT, E], F32).ap(),
        }
        with nc.Block() as block:
            @block.sync
            def _(sp):
                sp.dma_start(ident[:, :], io["ident"]).then_inc(ident_in, 16)
                sp.wait_ge(ident_in, 16)
        attend(nc, io, scr, mod, ident, rows, gated, ps)
        keep = {
            "w1": [sb(f"w1_{b}", [P, HID]) for b in range(RING)],
            "w2": [sb(f"w2_b1_{b}", [P, HID + HC]) for b in range(RING)],
            "b2": [sb(f"b2_rows{b}", [P, E]) for b in range(RING)],
            "spare_rows": sb("spare_rows", [P, BLOCKS * BT // P]),
            "x1": sb("x1", [P, NB, C, E]), "rows": rows, "block_expert": sb("block_expert", [P, BLOCKS], I32)}
        with ExitStack() as middle:
            sb = lambda n, s, d=F32: middle.enter_context(nc.sbuf_tensor(n, s, d))
            keep.update({
                "h2T": sb("h2T", [P, NB, S]), "h2_rows": sb("h2_rows", [P, T, E + 2]),
                "logits": sb("logits", [P, NB, C, NX]), "weight": sb("weight", [P, 2, T]),
                "slot": sb("slot", [P, 2, T], I32), "ids": sb("ids", [P, T]),
                "gate_b": sb("gate_b_rows", [P, NX]), "rank": sb("rank_rows", [P, NX]),
                "block_starts": sb("block_starts", [P, NB * S // BT]),
                "block_numbers": sb("block_numbers", [P, BLOCKS]), "upper": sb("upper", [P, P]),
                "bo_gated": gated[0], "wo_gated": gated[1],
            })
            merge(nc, io, scr, keep, mod, ident, ps)
            dispatch(nc, io, scr, keep, ps)
        experts(nc, io, scr, keep, ident, ps)
        combine(nc, io, scr, keep)


def kernel(**inputs):
    import numpy as np
    import concourse.bacc as bacc
    from concourse.bass_utils import run_bass_kernel_spmd

    a = {k[3:]: np.asarray(v) for k, v in inputs.items()}
    order = np.arange(E).reshape(H, D).T.reshape(-1)
    by_part = lambda w: w.reshape(NX, HC, P, E).transpose(0, 2, 1, 3).reshape(NX, P, HC * E)
    p, f32 = np.arange(P)[:, None], np.float32
    slot = (np.arange(BLOCKS)[:, None] * BT + np.arange(BT // P)).reshape(1, -1) + p * (BT // P)
    arrays = {
        "x": a["attn_x"], "cT": a["c"].T, "wmod": a["wmod"], "ident": np.eye(P, dtype=f32),
        "w_qkv": np.concatenate([a["attn_Wq"].T[:, order], a["attn_Wk"].T[:, order], a["attn_Wv"].T], 1),
        "b_qkv": np.concatenate([a["attn_bq"][order], a["attn_bk"][order], a["attn_bv"]]),
        "WoT": a["attn_Wo"].T, "bo": a["attn_bo"], "gate_w": a["ffn_gate_w"], "gate_b": a["ffn_gate_b"],
        "w1": a["ffn_w1"],
        "w2_pack": np.concatenate([by_part(a["ffn_w2"]), a["ffn_b1"].reshape(NX, HC, P).transpose(0, 2, 1)], 2),
        "b2": a["ffn_b2"], "ws1": a["ffn_ws1"], "ws2": a["ffn_ws2"],
        "bs1T": a["ffn_bs1"].reshape(HC, P).T, "bs2": a["ffn_bs2"],
        "rank": np.arange(NX, 0, -1).astype(f32), "upper": np.triu(np.ones((P, P), f32), 1),
        "block_starts": (np.arange(NB * S // BT) * BT).astype(f32), "block_numbers": np.arange(BLOCKS).astype(f32),
        "token_ids": (1 + np.arange(NB)[None, :, None] * S + p[:, :, None] * C
                      + np.arange(C)).reshape(P, -1).astype(f32),
        "spare_rows": (1 + 2 * NB * S + slot).astype(f32),
    }
    arrays = {k: np.ascontiguousarray(v) for k, v in arrays.items()}
    nc = bacc.Bacc("TRN2", target_bir_lowering=False, num_devices=1)
    io = {k: nc.dram_tensor(f"in_{k}", v.shape, mybir.dt.from_np(v.dtype), kind="ExternalInput").ap()
          for k, v in arrays.items()}
    out = nc.dram_tensor("out", (NB, S, E), F32, kind="ExternalOutput").ap()
    block_kernel(nc, io, out)
    r = run_bass_kernel_spmd(nc, [{f"in_{k}": v for k, v in arrays.items()}], core_ids=[0])
    return r.results[0]["out"]
```
